# Optimizing a Trainium2 kernel written in Bass

```python
import numpy as np
import jax
import jax.numpy as jnp

def _softmax(x, axis=-1):
    return jax.nn.softmax(x, axis=axis)

def _gelu(x):
    return jax.nn.gelu(x, approximate=True)

def _silu(x):
    return jax.nn.silu(x)

def _sigmoid(x):
    return jax.nn.sigmoid(x)

def _layernorm(x, axis=-1, eps=1e-05):
    m = jnp.mean(x, axis=axis, keepdims=True)
    v = jnp.var(x, axis=axis, keepdims=True)
    return (x - m) / jnp.sqrt(v + eps)

def _scatter_add(tgt, idx, src, axis=0):
    return tgt.at[idx].add(src)

def _segment_sum(src, seg, n):
    return jax.ops.segment_sum(src, seg, n)
kernel_name = 'mk_prb_d1_jaxref_r8_948615'

def setup_inputs(seed: int=0):
    np.random.seed(seed)
    _w = jnp.asarray

    def _L0_attn_setup():
        import jax, jax.numpy as jnp
        import numpy as np
        D_MODEL = 128
        N_HEADS = 16
        HEAD_DIM = D_MODEL // N_HEADS

        def _rope(x):
            B = x.shape[0]
            half = HEAD_DIM // 2
            theta = 1.0 / 10000.0 ** (jnp.arange(0, HEAD_DIM, 2, dtype=jnp.float32) / HEAD_DIM)
            pos = jnp.arange(B, dtype=jnp.float32)
            ang = pos[:, None] * theta[None, :]
            ang2 = jnp.concatenate([ang, ang], axis=-1)
            cos = jnp.cos(ang2)[:, None, None, :]
            sin = jnp.sin(ang2)[:, None, None, :]
            neg_half = jnp.concatenate([x[..., :half], -x[..., half:]], axis=-1)
            return x * cos + neg_half * sin
        key = jax.random.key(seed)
        k_x, k_q, k_k, k_v = jax.random.split(key, 4)
        B, S = (4, 256)
        scale = 1.0 / np.sqrt(D_MODEL)
        x = jax.random.normal(k_x, (B, S, D_MODEL), dtype=jnp.float32)
        Wq = jax.random.normal(k_q, (D_MODEL, D_MODEL), dtype=jnp.float32) * scale
        Wk = jax.random.normal(k_k, (D_MODEL, D_MODEL), dtype=jnp.float32) * scale
        Wv = jax.random.normal(k_v, (D_MODEL, D_MODEL), dtype=jnp.float32) * scale
        return {'x': x, 'Wq': Wq, 'Wk': Wk, 'Wv': Wv}
    _L0_attn_in = _L0_attn_setup()

    def _L0_ffn_setup():
        import jax, jax.numpy as jnp
        import numpy as np
        HIDDEN = 128
        MOE_INTER = 64
        SHARED_INTER = 256
        N_EXPERTS = 32
        TOP_K = 6
        N_GROUP = 8
        TOPK_GROUP = 4
        ROUTED_SCALE = 2.5

        def _relu2(x):
            return jnp.square(jax.nn.relu(x))

        def _router(x, gate_w, e_bias):
            T = x.shape[0]
            logits = x.astype(jnp.float32) @ gate_w.astype(jnp.float32).T
            scores = jax.nn.sigmoid(logits)
            sc = scores + e_bias[None, :]
            g = sc.reshape(T, N_GROUP, N_EXPERTS // N_GROUP)
            group_scores = jax.lax.top_k(g, 2)[0].sum(-1)
            group_idx = jax.lax.top_k(group_scores, TOPK_GROUP)[1]
            group_mask = jnp.zeros_like(group_scores).at[jnp.arange(T)[:, None], group_idx].set(1.0)
            score_mask = jnp.repeat(group_mask, N_EXPERTS // N_GROUP, axis=1)
            masked = jnp.where(score_mask > 0, sc, 0.0)
            topk_idx = jax.lax.stop_gradient(jax.lax.top_k(masked, TOP_K)[1])
            topk_w = jnp.take_along_axis(scores, topk_idx, axis=1)
            topk_w = topk_w / (topk_w.sum(-1, keepdims=True) + 1e-20)
            topk_w = topk_w * ROUTED_SCALE
            return (topk_idx, topk_w)
        if __name__ == '__main__':
            out = reference(**setup_inputs())
            print(out.shape, out.dtype)
        key = jax.random.key(seed)
        ks = jax.random.split(key, 6)
        s = 0.02
        return {'hidden_states': jax.random.normal(ks[0], (2, 128, HIDDEN), jnp.float32), 'gate_w': jax.random.normal(ks[1], (N_EXPERTS, HIDDEN), jnp.float32) * s, 'e_bias': jnp.zeros((N_EXPERTS,), jnp.float32), 'up_w': jax.random.normal(ks[2], (N_EXPERTS, MOE_INTER, HIDDEN), jnp.float32) * s, 'down_w': jax.random.normal(ks[3], (N_EXPERTS, HIDDEN, MOE_INTER), jnp.float32) * s, 'shared_up_w': jax.random.normal(ks[4], (SHARED_INTER, HIDDEN), jnp.float32) * s, 'shared_down_w': jax.random.normal(ks[5], (HIDDEN, SHARED_INTER), jnp.float32) * s}
    _L0_ffn_in = _L0_ffn_setup()
    _d = {'L0_attn_x': _L0_attn_in['x'], 'L0_attn_Wq': _L0_attn_in['Wq'], 'L0_attn_Wk': _L0_attn_in['Wk'], 'L0_attn_Wv': _L0_attn_in['Wv'], 'L0_ffn_gate_w': _L0_ffn_in['gate_w'], 'L0_ffn_e_bias': _L0_ffn_in['e_bias'], 'L0_ffn_up_w': _L0_ffn_in['up_w'], 'L0_ffn_down_w': _L0_ffn_in['down_w'], 'L0_ffn_shared_up_w': _L0_ffn_in['shared_up_w'], 'L0_ffn_shared_down_w': _L0_ffn_in['shared_down_w']}
    _x0 = _d['L0_attn_x']
    _d['L0_attn_x'] = jax.random.normal(jax.random.fold_in(jax.random.key(seed), 1), (8, 512, 128), dtype=_x0.dtype)
    del _x0
    return _d

def reference(L0_attn_x, L0_attn_Wq, L0_attn_Wk, L0_attn_Wv, L0_ffn_gate_w, L0_ffn_e_bias, L0_ffn_up_w, L0_ffn_down_w, L0_ffn_shared_up_w, L0_ffn_shared_down_w):

    def _L0_attn_ref(x, Wq, Wk, Wv):
        import jax, jax.numpy as jnp
        import numpy as np
        D_MODEL = 128
        N_HEADS = 16
        HEAD_DIM = D_MODEL // N_HEADS

        def _rope(x):
            B = x.shape[0]
            half = HEAD_DIM // 2
            theta = 1.0 / 10000.0 ** (jnp.arange(0, HEAD_DIM, 2, dtype=jnp.float32) / HEAD_DIM)
            pos = jnp.arange(B, dtype=jnp.float32)
            ang = pos[:, None] * theta[None, :]
            ang2 = jnp.concatenate([ang, ang], axis=-1)
            cos = jnp.cos(ang2)[:, None, None, :]
            sin = jnp.sin(ang2)[:, None, None, :]
            neg_half = jnp.concatenate([x[..., :half], -x[..., half:]], axis=-1)
            return x * cos + neg_half * sin
        B, S, D = x.shape
        q = (x @ Wq.T).reshape(B, S, N_HEADS, HEAD_DIM)
        k = (x @ Wk.T).reshape(B, S, N_HEADS, HEAD_DIM)
        v = (x @ Wv.T).reshape(B, S, N_HEADS, HEAD_DIM)
        q = _rope(q)
        k = _rope(k)
        q = q.transpose(0, 2, 1, 3)
        k = k.transpose(0, 2, 1, 3)
        v = v.transpose(0, 2, 1, 3)
        scores = jnp.einsum('bhqd,bhkd->bhqk', q, k) / np.sqrt(HEAD_DIM)
        weights = jax.nn.softmax(scores, axis=-1)
        out = jnp.einsum('bhqk,bhkd->bhqd', weights, v)
        return out.transpose(0, 2, 1, 3).reshape(B, S, D)

    def _L0_ffn_ref(hidden_states, gate_w, e_bias, up_w, down_w, shared_up_w, shared_down_w):
        import jax, jax.numpy as jnp
        import numpy as np
        HIDDEN = 128
        MOE_INTER = 64
        SHARED_INTER = 256
        N_EXPERTS = 32
        TOP_K = 6
        N_GROUP = 8
        TOPK_GROUP = 4
        ROUTED_SCALE = 2.5

        def _relu2(x):
            return jnp.square(jax.nn.relu(x))

        def _router(x, gate_w, e_bias):
            T = x.shape[0]
            logits = x.astype(jnp.float32) @ gate_w.astype(jnp.float32).T
            scores = jax.nn.sigmoid(logits)
            sc = scores + e_bias[None, :]
            g = sc.reshape(T, N_GROUP, N_EXPERTS // N_GROUP)
            group_scores = jax.lax.top_k(g, 2)[0].sum(-1)
            group_idx = jax.lax.top_k(group_scores, TOPK_GROUP)[1]
            group_mask = jnp.zeros_like(group_scores).at[jnp.arange(T)[:, None], group_idx].set(1.0)
            score_mask = jnp.repeat(group_mask, N_EXPERTS // N_GROUP, axis=1)
            masked = jnp.where(score_mask > 0, sc, 0.0)
            topk_idx = jax.lax.stop_gradient(jax.lax.top_k(masked, TOP_K)[1])
            topk_w = jnp.take_along_axis(scores, topk_idx, axis=1)
            topk_w = topk_w / (topk_w.sum(-1, keepdims=True) + 1e-20)
            topk_w = topk_w * ROUTED_SCALE
            return (topk_idx, topk_w)
        if __name__ == '__main__':
            out = reference(**setup_inputs())
            print(out.shape, out.dtype)
        B, S, H = hidden_states.shape
        x = hidden_states.reshape(-1, H)
        T = x.shape[0]
        topk_idx, topk_w = _router(x, gate_w, e_bias)
        combine = jnp.zeros((T, N_EXPERTS), topk_w.dtype).at[jnp.arange(T)[:, None], topk_idx].add(topk_w)
        h = _relu2(jnp.einsum('th,eih->tei', x, up_w))
        h = h * combine[:, :, None]
        moe_out = jnp.einsum('tei,ehi->th', h, down_w)
        shared = _relu2(x @ shared_up_w.T) @ shared_down_w.T
        return (moe_out + shared).reshape(B, S, H)
    x = L0_attn_x
    xn = _layernorm(x, axis=-1)
    x = x + _L0_attn_ref(xn, L0_attn_Wq, L0_attn_Wk, L0_attn_Wv) + _L0_ffn_ref(xn, L0_ffn_gate_w, L0_ffn_e_bias, L0_ffn_up_w, L0_ffn_down_w, L0_ffn_shared_up_w, L0_ffn_shared_down_w)
    return x

_drawn_inputs = setup_inputs


def setup_inputs(seed=0):
    import zlib

    import numpy as np

    out = dict(_drawn_inputs(seed))
    spreads = {'L0_ffn_e_bias': (0.0, 0.766)}
    factors = {'L0_ffn_gate_w': 7.839,
     'L0_ffn_up_w': 6.144,
     'L0_ffn_down_w': 5.59,
     'L0_ffn_shared_up_w': 3.086,
     'L0_ffn_shared_down_w': 2.8}
    for name, (base, spread) in spreads.items():
        noise = np.random.default_rng([zlib.crc32(name.encode()), seed]).standard_normal(out[name].shape)
        drawn = base * np.exp(spread * noise) if base else spread * noise
        out[name] = jnp.asarray(drawn.astype(out[name].dtype))
    for name, factor in factors.items():
        out[name] = (out[name] * factor).astype(out[name].dtype)
    return out
```

```python
from contextlib import ExitStack

import concourse.bass as bass
import numpy as np
from concourse import mybir

F32 = mybir.dt.float32
BF16 = mybir.dt.bfloat16
ALU = mybir.AluOpType
ACT = mybir.ActivationFunctionType
AXX = mybir.AxisListType.X

P = 128
B, T, D = 8, 512, 128
TT = T // P
NT = B * TT
H, HD = 16, 8
QUAD = 4
NQ = H // QUAD
NE, EI = 32, 64
SI = 256
NG, GE = 8, 4
TOPG, TOPK = 4, 6
ROUTED_SCALE = 2.5
SLICES = NE * EI // P
EPS = P // EI
NSH = SI // P
PARTS = 3
STACK = PARTS * PARTS * HD
ROWS = STACK + PARTS
VW = 32
LOW, MARK = -3.0e38, 3.0e38
EPS_LN = 1e-5
STORES = PARTS * PARTS + PARTS
LOADS = 1 + PARTS


def build(nc, x, wqT, wkT, wvT, gateT, e_bias, upT, down, shared_upT, shared_down, rope, ident_d, out):
    ctx = ExitStack()
    with ctx:
        def sb(name, shape, dt=F32):
            return ctx.enter_context(nc.sbuf_tensor(name, shape, dt))

        def sem(name):
            return ctx.enter_context(nc.semaphore(name))

        q_dram = nc.dram_tensor("q_stack", (H, PARTS, PARTS, HD, B * T), BF16).ap()
        k_dram = nc.dram_tensor("k_stack", (H, PARTS, HD, B * T), BF16).ap()

        x_in = sb("x_in", [P, NT, D])
        xnT = sb("xnT", [P, B * T])
        xcur = sb("xcur", [P, T])
        wq = sb("wq", [P, D]); wk = sb("wk", [P, D]); wv = sb("wv", [P, D])
        gate = sb("gate", [P, NE]); ebias = sb("ebias", [P, NE])
        up = sb("up", [P, NE * EI]); dn = sb("dn", [P, SLICES, D])
        sup = sb("sup", [P, SI]); sdn = sb("sdn", [P, NSH, D])
        fac = sb("fac", [P, 2 * B])
        ident = sb("ident", [P, P]); identb = sb("identb", [P, P], BF16)
        stats = sb("stats", [P, NT, 6]); mv = sb("mv", [P, NT, 2])
        ln = sb("ln", [P, 4, NT])
        qk32 = sb("qk32", [P, 2, B * T])
        qk_res = sb("qk_res", [P, 2, 2, T])
        qk_parts = sb("qk_parts", [P, 2, 2, PARTS, T], BF16)
        q_st = [sb(f"q_st{j}", [P, QUAD, T], BF16) for j in range(NQ)]
        k_st = [sb(f"k_st{j}", [P, QUAD, T], BF16) for j in range(NQ)]
        v_aug = sb("v_aug", [P, TT, H, VW])
        probs = sb("probs", [P, 2, QUAD, T])
        ffn = sb("ffn", [P, 4, 2, T])
        act_e = ffn[:, 0]
        g = ffn[:, 1]
        sh_r, sh_g = ffn[:, 2], ffn[:, 3]
        sqc = sb("sqc", [P, B, SLICES, TT, EPS])
        att_sb = sb("att_sb", [P, T])
        rec = sb("rec", [P, TT * QUAD])
        att_y = sb("att_y", [P, TT, NQ, QUAD * HD])
        y = sb("y", [P, 2, T])
        nmax = sb("nmax", [P, TT, QUAD]); nres = sb("nres", [P, 2, TT, QUAD])
        nparts = sb("nparts", [P, TT, PARTS, QUAD], BF16)
        mrow = sb("mrow", [PARTS * QUAD, T], BF16)
        xn = probs[:].rearrange("p a h t -> p (a h t)").rearrange("p (t d) -> p t d", d=D)
        sig = xn[:, 0:8, :].rearrange("p a b -> p (a b)").rearrange("p (t e) -> p t e", e=NE)
        sc = xn[:, 8:16, :].rearrange("p a b -> p (a b)").rearrange("p (t e) -> p t e", e=NE)
        tmp = xn[:, 16:24, :].rearrange("p a b -> p (a b)").rearrange("p (t e) -> p t e", e=NE)
        flat = ffn[:].rearrange("p a b t -> p (a b t)")
        room = [0]

        def scratch(*shape):
            at, room[0] = room[0], room[0] + shape[0] * shape[1]
            return flat[:, at:room[0]].rearrange("p (a b) -> p a b", b=shape[1])
        pair = scratch(6 * NT, NG).rearrange("p (n t) g -> p n t g", n=6)
        gsc = sb("gsc", [P, NT, NG + TOPG]); gtop = sb("gtop", [P, NT, 8])
        gmark = sb("gmark", [P, NT, NG + TOPG])
        msk = scratch(NT, NE + 2); etop = sb("etop", [P, NT, 8]); emark = scratch(NT, NE + 2)
        wsum = sb("wsum", [P, 2, NT])

        bank = [ctx.enter_context(nc.psum_tensor(n, [P, 512], F32))
                for n in ("sc0", "sc1", "st0", "st1", "pv", "upb", "tr", "acc")]
        sc_b, st_b, pv_b, up_b, tr_b, acc_b = bank[0:2], bank[2:4], bank[4], bank[5], bank[6], bank[7]

        pool_waited = sem("pool_waited")
        x_ld = [sem(f"x_ld{i}") for i in range(B)]
        w_ld = sem("w_ld"); w2_ld = sem("w2_ld")
        set_ready = sem("set_ready")
        link = sem("link")
        var_ready = sem("var_ready"); std_ready = sem("std_ready")
        xn_ready = sem("xn_ready"); xnT_psum = sem("xnT_psum"); xnT_ready = sem("xnT_ready")
        logit_ready = sem("logit_ready"); sig_ready = sem("sig_ready")
        gw_ready = sem("gw_ready"); sqc_ready = sem("sqc_ready")
        proj_ready = sem("proj_ready"); qk32_ready = sem("qk32_ready")
        split_step = sem("split_step"); parts_ready = sem("parts_ready")
        stored = [sem("stored0"), sem("stored1")]
        st_ld = [sem(f"st_ld{j}") for j in range(NQ)]
        s_done = sem("s_done"); s_read = sem("s_read")
        neg_step = sem("neg_step"); negmax_ready = sem("negmax_ready")
        mrow_ready = sem("mrow_ready"); mrow_ld = sem("mrow_ld")
        t_done = sem("t_done"); probs_ready = sem("probs_ready")
        pv_done = sem("pv_done"); att_ready = sem("att_ready")
        up_done = sem("up_done"); v_ready = sem("v_ready"); act_ready = sem("act_ready")
        tr_done = sem("tr_done"); g_ready = sem("g_ready")
        xcur_ready = sem("xcur_ready"); sh_relu = sem("sh_relu"); sh_ready = sem("sh_ready")
        down_done = sem("down_done"); rec_ready = sem("rec_ready"); atty_ready = sem("atty_ready")
        sum_ready = sem("sum_ready"); y_ready = sem("y_ready"); y_stored = sem("y_stored")

        def score_heads(kt, slot):
            return ((2, 1, 1, 2), (1, 1, 1, 2), (1, 2, 1, 1), (0, 0, 0, 0))[kt][slot]

        def up_units():
            order = [("v", 0)]
            for n in range(SLICES):
                if n < NSH:
                    order.append(("shared", n))
                order.append(("slice", n))
            return {u: n for n, u in enumerate(order)}
        UP = up_units()
        NUP = len(UP)

        def tr_units(last):
            order = []
            for j in range(NQ):
                for kt in range(TT):
                    if kt == TT - 1 and not (last and j == NQ - 1):
                        order.append(("max", j))
                    if kt == 1 and j:
                        order.append(("att", j - 1))
                    order.append(("slice", j * TT + kt))
            order.append(("att", NQ - 1))
            return {u: n for n, u in enumerate(order)}
        NTR = len(tr_units(False))

        def tr_count(b, last, kind, n):
            return 1 + b * NTR + tr_units(last)[kind, n] + 1

        NDOWN = SLICES + NSH

        def wait(eng, semaphore, count):
            if not isinstance(count, int) or count > 0:
                eng.wait_ge(semaphore, count)

        def over_batches(eng, body):
            body(0, False)
            with eng.Fori(1, B - 1) as b:
                body(b, False)
            body(B - 1, True)

        block = ctx.enter_context(nc.Block())

        @block.sync
        def _(sp):
            for i in range(B):
                sp.dma_start(x_in[:, i * TT:(i + 1) * TT, :],
                             x[i * T:(i + 1) * T, :].rearrange("(t p) d -> p t d", p=P)).then_inc(x_ld[i], 16)
            for dst, src in ((ident, ident_d), (wq, wqT), (wk, wkT), (fac, rope), (gate, gateT)):
                sp.dma_start(dst[:], src).then_inc(w_ld, 16)
            sp.dma_start(ebias[:], e_bias.partition_broadcast(P)).then_inc(w_ld, 16)
            sp.dma_start(wv[:], wvT).then_inc(w2_ld, 16)
            sp.dma_start(sup[:], shared_upT).then_inc(w2_ld, 16)
            sp.dma_start(up[:], upT).then_inc(w2_ld, 16)
            sp.dma_start(sdn[:], shared_down.rearrange("(n p) d -> p n d", p=P)).then_inc(w2_ld, 16)
            sp.dma_start(dn[:], down.rearrange("(n p) d -> p n d", p=P)).then_inc(w2_ld, 16)

            with sp.Fori(0, B // 2) as bb:
                for par in range(2):
                    b = bb * 2 + par
                    t_at = bass.ds(bb * (2 * T) + par * T, T)
                    sp.wait_ge(parts_ready, b * 2 + 1)
                    for i in range(PARTS):
                        for r in range(PARTS):
                            sp.dma_start(q_dram[:, i, r, :, t_at],
                                         qk_parts[:, par, 0, i, :]).then_inc(stored[par], 16)
                    sp.wait_ge(parts_ready, b * 2 + 2)
                    for i in range(PARTS):
                        sp.dma_start(k_dram[:, i, :, t_at], qk_parts[:, par, 1, i, :]).then_inc(stored[par], 16)

            def load_stack(b, j):
                heads = slice(j * QUAD, (j + 1) * QUAD)
                t_at = bass.ds(b * T, T)
                sp.dma_start(q_st[j][0:STACK, :, :],
                             q_dram[heads, :, :, :, t_at].rearrange("h i r d t -> (i r d) h t")
                             ).then_inc(st_ld[j], 16)
                for i in range(PARTS):
                    rows = slice(i * PARTS * HD, (i + 1) * PARTS * HD)
                    sp.dma_start(k_st[j][rows, :, :],
                                 k_dram[heads, :, :, t_at].rearrange("h r d t -> (r d) h t")
                                 ).then_inc(st_ld[j], 16)

            def load_max(step, j):
                sp.wait_ge(mrow_ready, step + 1)
                sp.dma_start(q_st[j][STACK:ROWS, :, :],
                             mrow[:, :]).then_inc(mrow_ld, 16)

            sp.wait_ge(set_ready, 2)
            for par in range(2):
                sp.wait_ge(stored[par], B // 2 * STORES * 16)
            for j in range(NQ):
                load_stack(0, j)
            load_max(0, 0)

            def batch(b, last):
                for j in range(NQ):
                    if not (last and j == NQ - 1):
                        load_max(b * NQ + j + 1, (j + 1) % NQ)
                    if not last:
                        sp.wait_ge(t_done, (b * NQ + j + 1) * TT * QUAD)
                        load_stack(b + 1, j)
                sp.wait_ge(y_ready, b + 1)
                sp.dma_start(out[bass.ds(b * T, T), :].rearrange("(t p) d -> p t d", p=P),
                             y[:, 1, :].rearrange("p (t d) -> p t d", d=D)).then_inc(y_stored, 16)
            over_batches(sp, batch)
            sp.wait_ge(y_stored, B * 16)

        @block.gpsimd
        def _(pool):
            def plain():
                nc.gpsimd.sem_inc(pool_waited, 1)

            def cut_two(bb):
                for par in range(2):
                    for w in range(2):
                        n = (bb * 2 + par) * 2 + w
                        src = qk32[:, w, bass.ds(bb * (2 * T) + par * T, T)]
                        res = qk_res[:, w, :, :]
                        part = qk_parts[:, par, w, :, :]
                        pool.wait_ge(qk32_ready, n + 1)
                        if w == 0:
                            wait(pool, stored[par], bb * (STORES * 16))
                        plain()
                        nc.gpsimd.tensor_copy(part[:, 0, :], src).then_inc(split_step, 1)
                        pool.wait_ge(split_step, n * 4 + 1)
                        plain()
                        nc.gpsimd.tensor_tensor(res[:, 0, :], src, part[:, 0, :], ALU.subtract).then_inc(split_step, 1)
                        pool.wait_ge(split_step, n * 4 + 2)
                        plain()
                        nc.gpsimd.tensor_copy(part[:, 1, :], res[:, 0, :]).then_inc(split_step, 1)
                        pool.wait_ge(split_step, n * 4 + 3)
                        plain()
                        nc.gpsimd.tensor_tensor(res[:, 1, :], res[:, 0, :], part[:, 1, :],
                                                ALU.subtract).then_inc(split_step, 1)
                        pool.wait_ge(split_step, n * 4 + 4)
                        plain()
                        nc.gpsimd.tensor_copy(part[:, 2, :], res[:, 1, :]).then_inc(parts_ready, 1)
            cut_two(0)
            with pool.Fori(1, B // 2) as bb:
                cut_two(bb)

            def batch(b, last):
                wait(pool, up_done, b * NUP)
                plain()
                nc.gpsimd.tensor_copy(xcur[:], xnT[:, bass.ds(b * T, T)]).then_inc(xcur_ready, 1)
                for i in range(NSH):
                    wait(pool, sh_relu, b * NSH + i + 1)
                    wait(pool, down_done, b * NDOWN)
                    plain()
                    nc.gpsimd.tensor_tensor(sh_g[:, i, :], sh_r[:, i, :], sh_r[:, i, :],
                                            ALU.mult).then_inc(sh_ready, 1)
            pool.wait_ge(xnT_ready, B)
            over_batches(pool, batch)

        @block.scalar
        def _(act):
            act.wait_ge(var_ready, 1)
            nc.scalar.activation(ln[:, 1, :], ln[:, 0, :], ACT.Sqrt).then_inc(std_ready, 1)
            for i in range(B):
                act.wait_ge(xnT_psum, i + 1)
                nc.scalar.activation(xnT[:, i * T:(i + 1) * T], bank[5 + i % 2][:], ACT.Copy).then_inc(xnT_ready, 1)
            for i in range(2):
                act.wait_ge(logit_ready, i + 1)
                nc.scalar.activation(sig[:, i * NT // 2:(i + 1) * NT // 2, :].rearrange("p t e -> p (t e)"),
                                     bank[2 + i][:], ACT.Sigmoid).then_inc(sig_ready, 1)
            with act.Fori(0, B) as b:
                for w in range(2):
                    wait(act, proj_ready, b * 2 + w + 1)
                    nc.scalar.activation(qk32[:, w, bass.ds(b * T, T)], bank[w][:], ACT.Copy,
                                         scale=fac[:, bass.ds(b * 2 + w, 1)]).then_inc(qk32_ready, 1)
            act.wait_ge(gw_ready, 1)
            for b in range(B):
                nc.scalar.activation(sqc[:, b, :, :, :].rearrange("p n t e -> p t n e"),
                                     tmp[:, b * TT:(b + 1) * TT, :].rearrange("p t (n e) -> p t n e", e=EPS),
                                     ACT.Sqrt).then_inc(sqc_ready, 1)

            act.wait_ge(set_ready, 1)

            def batch(b, last):
                for j in range(NQ):
                    for kt in range(TT):
                        n = j * TT + kt
                        for h in range(QUAD):
                            i = b * (SLICES * QUAD) + n * QUAD + h
                            act.wait_ge(t_done, i + 1)
                            if h == 0:
                                if n >= 2:
                                    wait(act, pv_done, b * SLICES + n - 1)
                                else:
                                    wait(act, pv_done, b * SLICES)
                            nc.scalar.activation(probs[:, kt % 2, h, :], st_b[h % 2][:], ACT.Exp
                                                 ).then_inc(probs_ready, 1)
                            if n == 0 and h == 0:
                                wait(act, up_done, b * NUP + UP["v", 0] + 1)
                                nc.scalar.activation(v_aug[:, :, :, 0:HD],
                                                     up_b[:].rearrange("p (t h d) -> p t h d", t=TT, h=H),
                                                     ACT.Copy).then_inc(v_ready, 1)
                            if n < NSH and h == 0:
                                wait(act, up_done, b * NUP + UP["shared", n] + 1)
                                wait(act, sh_ready, b * NSH)
                                nc.scalar.activation(sh_r[:, n, :], up_b[:], ACT.Relu).then_inc(sh_relu, 1)
                            if h == QUAD - 1:
                                act.wait_ge(tr_done, tr_count(b, last, "slice", n))
                                wait(act, down_done, b * NDOWN + max(n - 1, 0))
                                nc.scalar.activation(g[:, n % 2, :], tr_b[:], ACT.Square).then_inc(g_ready, 1)
            over_batches(act, batch)

        @block.vector
        def _(dve):
            done = [0]

            def then(ins):
                done[0] += 1
                ins.then_inc(link, 1)
                dve.wait_ge(link, done[0])

            then(nc.vector.memset(v_aug[:], 0.0))
            nc.vector.memset(v_aug[:, :, :, HD:HD + 1], 1.0).then_inc(set_ready, 1)
            for j in range(NQ):
                last = nc.vector.memset(k_st[j][64:96, :, :], 1.0)
            last.then_inc(set_ready, 1)
            for i in range(B):
                dve.wait_ge(x_ld[i], 16)
                for t in range(i * TT, (i + 1) * TT):
                    last = nc.vector.bn_stats(stats[:, t, :], x_in[:, t, :])
            then(last)
            for t in range(NT):
                last = nc.vector.bn_aggr(mv[:, t, :], stats[:, t, :])
            then(last)
            then(nc.vector.tensor_scalar_add(ln[:, 0, :], mv[:, :, 1], EPS_LN))
            nc.vector.memset(gsc[:, :, NG:], LOW)
            last = nc.vector.memset(msk[:, :, NE:], LOW)
            last.then_inc(var_ready, 1)
            dve.wait_ge(std_ready, 1)
            then(nc.vector.reciprocal(ln[:, 2, :], ln[:, 1, :]))
            then(nc.vector.tensor_tensor(ln[:, 3, :], ln[:, 0, :], ln[:, 2, :], ALU.mult))
            then(nc.vector.tensor_tensor(ln[:, 2, :], ln[:, 3, :], ln[:, 1, :], ALU.add))
            then(nc.vector.tensor_scalar(ln[:, 3, :], ln[:, 2, :], 0.5, None, ALU.mult))
            then(nc.vector.reciprocal(ln[:, 1, :], ln[:, 3, :]))
            for i in range(B):
                for t in range(i * TT, (i + 1) * TT):
                    last = nc.vector.tensor_scalar(xn[:, t, :], x_in[:, t, :], mv[:, t, 0:1], ln[:, 1, t:t + 1],
                                                   ALU.subtract, ALU.mult)
                last.then_inc(xn_ready, 1)

            dve.wait_ge(sig_ready, 2)
            dve.wait_ge(w_ld, 6 * 16)
            then(nc.vector.tensor_tensor(sc, sig, ebias[:, :].unsqueeze(1).to_broadcast([P, NT, NE]), ALU.add))
            e4 = sc.rearrange("p t (g e) -> p t g e", e=GE)
            pr = lambda n: pair[:, n, :, :]
            nc.vector.tensor_tensor(pr(0), e4[:, :, :, 0], e4[:, :, :, 1], ALU.max)
            nc.vector.tensor_tensor(pr(1), e4[:, :, :, 0], e4[:, :, :, 1], ALU.min)
            nc.vector.tensor_tensor(pr(2), e4[:, :, :, 2], e4[:, :, :, 3], ALU.max)
            then(nc.vector.tensor_tensor(pr(3), e4[:, :, :, 2], e4[:, :, :, 3], ALU.min))
            nc.vector.tensor_tensor(pr(4), pr(0), pr(2), ALU.min)
            then(nc.vector.tensor_tensor(pr(5), pr(1), pr(3), ALU.max))
            nc.vector.tensor_tensor(pr(1), pr(0), pr(2), ALU.max)
            then(nc.vector.tensor_tensor(pr(3), pr(4), pr(5), ALU.max))
            then(nc.vector.tensor_tensor(gsc[:, :, 0:NG], pr(1), pr(3), ALU.add))
            for t in range(NT):
                last = nc.vector.max(out=gtop[:, t, :], in_=gsc[:, t, 0:NG])
            then(last)
            then(nc.vector.memset(gtop[:, :, TOPG:], LOW))
            for t in range(NT):
                last = nc.vector.match_replace(out=gmark[:, t, :], in_to_replace=gtop[:, t, :],
                                               in_values=gsc[:, t, :], imm_value=MARK)
            then(last)
            then(nc.vector.tensor_scalar(pr(0), gmark[:, :, 0:NG], MARK, None, ALU.is_equal))
            then(nc.vector.tensor_tensor(tmp.rearrange("p t (g e) -> p t g e", e=GE), e4,
                                         pr(0).unsqueeze(3).to_broadcast([P, NT, NG, GE]), ALU.mult))
            then(nc.vector.tensor_scalar_add(msk[:, :, 0:NE], tmp, 0.0))
            for t in range(NT):
                last = nc.vector.max(out=etop[:, t, :], in_=msk[:, t, 0:NE])
            then(last)
            then(nc.vector.memset(etop[:, :, TOPK:], LOW))
            for t in range(NT):
                last = nc.vector.match_replace(out=emark[:, t, :], in_to_replace=etop[:, t, :],
                                               in_values=msk[:, t, :], imm_value=MARK)
            then(last)
            then(nc.vector.tensor_scalar(sc, emark[:, :, 0:NE], MARK, None, ALU.is_equal))
            then(nc.vector.tensor_tensor(tmp, sc, sig, ALU.mult))
            then(nc.vector.tensor_reduce(out=wsum[:, 0, :], in_=tmp, op=ALU.add, axis=AXX))
            then(nc.vector.tensor_scalar_add(wsum[:, 1, :], wsum[:, 0, :], 1e-20))
            then(nc.vector.reciprocal(wsum[:, 0, :], wsum[:, 1, :]))
            then(nc.vector.tensor_scalar(wsum[:, 1, :], wsum[:, 0, :], ROUTED_SCALE, None, ALU.mult))
            nc.vector.tensor_tensor(tmp, tmp, wsum[:, 1, :].unsqueeze(2).to_broadcast([P, NT, NE]),
                                    ALU.mult).then_inc(gw_ready, 1)

            def row_max(step, i):
                dve.wait_ge(s_done, step * (TT * QUAD) + i + 1)
                nc.vector.tensor_reduce(out=nmax[:, i % TT, i // TT:i // TT + 1], in_=sc_b[i % 2][:],
                                        op=ALU.max, axis=AXX, negate=True).then_inc(s_read, 1)

            def cut_max(step):
                dve.wait_ge(s_read, (step + 1) * TT * QUAD)
                nc.vector.tensor_copy(nparts[:, :, 0, :], nmax[:]).then_inc(neg_step, 1)
                dve.wait_ge(neg_step, step * 4 + 1)
                nc.vector.tensor_tensor(nres[:, 0], nmax[:], nparts[:, :, 0, :], ALU.subtract).then_inc(neg_step, 1)
                dve.wait_ge(neg_step, step * 4 + 2)
                nc.vector.tensor_copy(nparts[:, :, 1, :], nres[:, 0]).then_inc(neg_step, 1)
                dve.wait_ge(neg_step, step * 4 + 3)
                nc.vector.tensor_tensor(nres[:, 1], nres[:, 0], nparts[:, :, 1, :], ALU.subtract).then_inc(neg_step, 1)
                dve.wait_ge(neg_step, step * 4 + 4)
                nc.vector.tensor_copy(nparts[:, :, 2, :], nres[:, 1]).then_inc(negmax_ready, 1)

            def max_rows(step, count):
                dve.wait_ge(tr_done, count)
                wait(dve, mrow_ld, step * 16)
                nc.vector.tensor_copy(mrow[:, :], tr_b[:].bitcast(BF16)[0:PARTS * QUAD, 0:T]).then_inc(mrow_ready, 1)

            nc.vector.tensor_copy(identb[:], ident[:])
            for i in range(TT * QUAD):
                row_max(0, i)
            cut_max(0)
            max_rows(0, 1)
            dve.wait_ge(sqc_ready, B)

            def batch(b, last):
                def att_out(j):
                    dve.wait_ge(tr_done, tr_count(b, last, "att", j))
                    a4 = tr_b[:].rearrange("p (n c) -> p n c", c=VW)
                    nc.vector.reciprocal(rec[:].unsqueeze(2), a4[:, :, HD:HD + 1]).then_inc(rec_ready, 1)
                    wait(dve, rec_ready, b * NQ + j + 1)
                    nc.vector.tensor_tensor(att_y[:, :, j, :].rearrange("p t (h d) -> p t h d", d=HD),
                                            a4[:, :, 0:HD].rearrange("p (t h) d -> p t h d", h=QUAD),
                                            rec[:].rearrange("p (t h) -> p t h", h=QUAD).unsqueeze(3)
                                            .to_broadcast([P, TT, QUAD, HD]), ALU.mult).then_inc(atty_ready, 1)

                def att_evac(j):
                    wait(dve, pv_done, b * SLICES + (j + 1) * TT)
                    nc.vector.tensor_copy(att_sb[:], pv_b[:]).then_inc(att_ready, 1)

                i = 0
                for j in range(NQ):
                    step = b * NQ + j + 1
                    skip = last and j == NQ - 1
                    i = 0
                    for kt in range(TT):
                        n = j * TT + kt
                        for slot in range(QUAD):
                            if kt == TT - 1 and slot == 0 and not skip:
                                cut_max(step)
                            if not skip:
                                for _ in range(score_heads(kt, slot)):
                                    row_max(step, i)
                                    i += 1
                            if slot == 0:
                                wait(dve, up_done, b * NUP + UP["slice", n] + 1)
                                if n >= 2:
                                    dve.wait_ge(tr_done, tr_count(b, last, "slice", n - 2))
                                nc.vector.scalar_tensor_tensor(
                                    out=act_e[:, n % 2, :].rearrange("p (m i) -> p m i", i=EI),
                                    in0=up_b[:].rearrange("p (m i) -> p m i", i=EI), scalar=0.0,
                                    in1=sqc[:, bass.ds(b, 1), n, :, :].rearrange("p o t e -> p (o t e)").unsqueeze(2)
                                    .to_broadcast([P, TT * EPS, EI]),
                                    op0=ALU.max, op1=ALU.mult).then_inc(act_ready, 1)
                                if kt == TT - 1 and not skip:
                                    max_rows(step, tr_count(b, last, "max", j))
                            if slot == 1 and kt == 0 and j:
                                att_evac(j - 1)
                            if slot == 1 and kt == 1 and j:
                                att_out(j - 1)
                att_evac(NQ - 1)
                att_out(NQ - 1)
                wait(dve, down_done, (b + 1) * NDOWN)
                wait(dve, atty_ready, (b + 1) * NQ)
                nc.vector.tensor_tensor(y[:, 0, :], acc_b[:], att_y[:].rearrange("p t j c -> p (t j c)"),
                                        ALU.add).then_inc(sum_ready, 1)
                wait(dve, sum_ready, b + 1)
                wait(dve, y_stored, b * 16)
                nc.vector.tensor_tensor(y[:, 1, :], y[:, 0, :],
                                        x_in[:, bass.ds(b * TT, TT), :].rearrange("p t d -> p (t d)"),
                                        ALU.add).then_inc(y_ready, 1)
            over_batches(dve, batch)

        @block.tensor
        def _(pe):
            pe.wait_ge(w_ld, 6 * 16)
            for i in range(B):
                pe.wait_ge(xn_ready, i + 1)
                if i >= 2:
                    pe.wait_ge(xnT_ready, i - 1)
                for t in range(TT):
                    last = nc.tensor.transpose(bank[5 + i % 2][:, t * P:(t + 1) * P], xn[:, i * TT + t, :], ident[:])
                last.then_inc(xnT_psum, 1)
            pe.wait_ge(xnT_ready, B)
            for i in range(2):
                for t in range(NT // 2):
                    tile = i * NT // 2 + t
                    last = nc.tensor.matmul(bank[2 + i][:, t * NE:(t + 1) * NE], xnT[:, tile * P:(tile + 1) * P],
                                            gate[:], start=True, stop=True)
                last.then_inc(logit_ready, 1)
            def project(b):
                for w, weights in enumerate((wq, wk)):
                    wait(pe, qk32_ready, b * 2)
                    nc.tensor.matmul(bank[w][:], weights[:], xnT[:, bass.ds(b * T, T)],
                                     start=True, stop=True).then_inc(proj_ready, 1)
            project(0)
            with pe.Fori(1, B) as b:
                project(b)

            def score(step, j, i):
                h, qt = i // TT, i % TT
                nc.tensor.matmul(sc_b[i % 2][:], q_st[j][0:STACK, h, qt * P:(qt + 1) * P], k_st[j][0:STACK, h, :],
                                 start=True, stop=True).then_inc(s_done, 1)

            def max_transpose(step):
                pe.wait_ge(negmax_ready, step + 1)
                for qt in range(TT):
                    last = nc.tensor.transpose(tr_b[:].bitcast(BF16)[0:PARTS * QUAD, qt * P:(qt + 1) * P],
                                               nparts[:, qt, :, :].rearrange("p i h -> p (i h)"), identb[:])
                last.then_inc(tr_done, 1)

            pe.wait_ge(qk32_ready, 2 * B)
            pe.wait_ge(st_ld[0], LOADS * 16)
            for i in range(TT * QUAD):
                if i >= 2:
                    pe.wait_ge(s_read, i - 1)
                score(0, 0, i)
            pe.wait_ge(w2_ld, 5 * 16)
            max_transpose(0)
            pe.wait_ge(sig_ready, 2)

            def batch(b, last):
                def read_before(eng_unit):
                    kind, n = eng_unit
                    if kind == "v":
                        wait(pe, v_ready, b + 1)
                    elif kind == "shared":
                        wait(pe, sh_relu, b * NSH + n + 1)
                    elif kind == "up":
                        wait(pe, act_ready, b * SLICES + n + 1)
                    elif kind == "square":
                        wait(pe, g_ready, b * SLICES + n + 1)
                    elif kind == "max":
                        wait(pe, mrow_ready, b * NQ + n + 2)
                    elif kind == "att":
                        wait(pe, atty_ready, b * NQ + n + 1)

                def pv(n):
                    j, kt = n // TT, n % TT
                    wait(pe, probs_ready, (b * SLICES + n + 1) * QUAD)
                    if kt == 0:
                        wait(pe, att_ready, b * NQ + j)
                    for h in range(QUAD):
                        m = nc.tensor.matmul(pv_b[h * VW:(h + 1) * VW, :], v_aug[:, kt, j * QUAD + h, :],
                                             probs[:, kt % 2, h, :], start=kt == 0, stop=kt == TT - 1)
                    m.then_inc(pv_done, 1)

                def down_slice(src, weights, first, end):
                    for t in range(TT):
                        m = nc.tensor.matmul(acc_b[:, t * P:(t + 1) * P], src[:, t * P:(t + 1) * P], weights,
                                             start=first and t == 0, stop=end, skip_group_check=True)
                    m.then_inc(down_done, 1)

                def down(n):
                    wait(pe, g_ready, b * SLICES + n + 1)
                    if n == 0:
                        pe.wait_ge(sum_ready, b)
                    down_slice(g[:, n % 2, :], dn[:, n, :], n == 0, n == SLICES - 1)

                def down_shared(i):
                    wait(pe, sh_ready, b * NSH + i + 1)
                    down_slice(sh_g[:, i, :], sdn[:, i, :], False, False)

                def att_transpose(j):
                    wait(pe, att_ready, b * NQ + j + 1)
                    for t in range(TT):
                        m = nc.tensor.transpose(tr_b[:, t * P:(t + 1) * P], att_sb[:, t * P:(t + 1) * P], ident[:])
                    m.then_inc(tr_done, 1)

                tr_user = None
                for j in range(NQ):
                    step = b * NQ + j + 1
                    nxt = (j + 1) % NQ
                    skip = last and j == NQ - 1
                    i = 0
                    for kt in range(TT):
                        n = j * TT + kt
                        for h in range(QUAD):
                            at = n * QUAD + h
                            if kt == 0 and h == 0:
                                wait(pe, mrow_ld, (b * NQ + j + 1) * 16)
                            wait(pe, probs_ready, b * (SLICES * QUAD) + (at - 1 if at >= 2 else 0))
                            nc.tensor.matmul(st_b[h % 2][:], k_st[j][0:ROWS, h, kt * P:(kt + 1) * P],
                                             q_st[j][0:ROWS, h, :], start=True, stop=True).then_inc(t_done, 1)
                            if not skip:
                                for _ in range(score_heads(kt, h)):
                                    if i == 0:
                                        pe.wait_ge(st_ld[nxt], (b + (2 if nxt == 0 else 1)) * (LOADS * 16))
                                    pe.wait_ge(s_read, step * (TT * QUAD) + i - 1)
                                    score(step, nxt, i)
                                    i += 1
                            if h == 0:
                                if n == 0:
                                    wait(pe, xcur_ready, b + 1)
                                    wait(pe, act_ready, b * SLICES)
                                    for t in range(TT):
                                        m = nc.tensor.matmul(up_b[:, t * P:(t + 1) * P], xcur[:, t * P:(t + 1) * P],
                                                             wv[:], start=True, stop=True)
                                    m.then_inc(up_done, 1)
                                if n < NSH:
                                    read_before(("v", 0) if n == 0 else ("up", n - 1))
                                    nc.tensor.matmul(up_b[:], sup[:, n * P:(n + 1) * P], xcur[:],
                                                     start=True, stop=True).then_inc(up_done, 1)
                                read_before(("shared", n) if n < NSH else ("up", n - 1))
                                for t in range(TT):
                                    m = nc.tensor.matmul(up_b[:, t * P:(t + 1) * P], xcur[:, t * P:(t + 1) * P],
                                                         up[:, n * P:(n + 1) * P], start=True, stop=True)
                                m.then_inc(up_done, 1)
                                if kt == TT - 1 and not skip:
                                    read_before(tr_user)
                                    max_transpose(step)
                                    tr_user = ("max", j)
                            elif h == 1:
                                if n:
                                    pv(n - 1)
                                if kt == 1 and j:
                                    read_before(tr_user)
                                    att_transpose(j - 1)
                                    tr_user = ("att", j - 1)
                            elif h == 2:
                                if n:
                                    down(n - 1)
                            else:
                                if tr_user:
                                    read_before(tr_user)
                                else:
                                    wait(pe, atty_ready, b * NQ)
                                    pe.wait_ge(mrow_ready, 1)
                                wait(pe, act_ready, b * SLICES + n + 1)
                                for t in range(TT):
                                    m = nc.tensor.transpose(tr_b[:, t * P:(t + 1) * P],
                                                            act_e[:, n % 2, t * P:(t + 1) * P], ident[:])
                                m.then_inc(tr_done, 1)
                                tr_user = ("square", n)
                down_shared(0)
                pv(SLICES - 1)
                down_shared(1)
                down(SLICES - 1)
                read_before(tr_user)
                att_transpose(NQ - 1)
            over_batches(pe, batch)


def kernel(L0_attn_x, L0_attn_Wq, L0_attn_Wk, L0_attn_Wv, L0_ffn_gate_w, L0_ffn_e_bias, L0_ffn_up_w,
           L0_ffn_down_w, L0_ffn_shared_up_w, L0_ffn_shared_down_w):
    from concourse import bacc
    from concourse.bass_utils import run_bass_kernel_spmd

    half = HD // 2
    theta = 1.0 / 10000.0 ** (np.arange(0, HD, 2, dtype=np.float64) / HD)
    angle = np.arange(B, dtype=np.float64)[:, None] * theta[None, :]
    turn = np.concatenate([np.cos(angle) + np.sin(angle), np.cos(angle) - np.sin(angle)], axis=1)
    assert turn.shape == (B, 2 * half)
    rope = np.tile(np.stack([turn / np.sqrt(HD), turn], axis=1).reshape(2 * B, HD).T, (H, 1)).astype(np.float32)

    def lay(a):
        return np.ascontiguousarray(a)

    x = np.asarray(L0_attn_x)
    arrays = {
        "x": lay(x.reshape(B * T, D)),
        "wqT": lay(np.asarray(L0_attn_Wq).T),
        "wkT": lay(np.asarray(L0_attn_Wk).T),
        "wvT": lay(np.asarray(L0_attn_Wv).T),
        "gateT": lay(np.asarray(L0_ffn_gate_w).T),
        "e_bias": lay(np.asarray(L0_ffn_e_bias)),
        "upT": lay(np.asarray(L0_ffn_up_w).reshape(NE * EI, D).T),
        "down": lay(np.asarray(L0_ffn_down_w).transpose(0, 2, 1).reshape(NE * EI, D)),
        "shared_upT": lay(np.asarray(L0_ffn_shared_up_w).T),
        "shared_down": lay(np.asarray(L0_ffn_shared_down_w).T),
        "rope": lay(rope),
        "ident_d": np.eye(P, dtype=np.float32),
    }
    nc = bacc.Bacc("TRN2", target_bir_lowering=False, num_devices=1)
    args = [nc.dram_tensor(f"in_{n}", a.shape, mybir.dt.from_np(a.dtype), kind="ExternalInput").ap()
            for n, a in arrays.items()]
    out = nc.dram_tensor("out", (B * T, D), F32, kind="ExternalOutput").ap()
    build(nc, *args, out)
    r = run_bass_kernel_spmd(nc, [{f"in_{n}": a for n, a in arrays.items()}], core_ids=[0])
    return r.results[0]["out"].reshape(B, T, D)
```

```python
from contextlib import ExitStack

import concourse.bass as bass
import numpy as np
from concourse import mybir

F32 = mybir.dt.float32
BF16 = mybir.dt.bfloat16
ALU = mybir.AluOpType
ACT = mybir.ActivationFunctionType
AXX = mybir.AxisListType.X

P = 128
B, T, D = 8, 512, 128
TT = T // P
NT = B * TT
H, HD = 16, 8
QUAD = 4
NQ = H // QUAD
NE, EI = 32, 64
SI = 256
NG, GE = 8, 4
TOPG, TOPK = 4, 6
ROUTED_SCALE = 2.5
SLICES = NE * EI // P
EPS = P // EI
NSH = SI // P
PARTS = 3
STACK = PARTS * PARTS * HD
ROWS = STACK + PARTS
VW = 32
LOW, MARK = -3.0e38, 3.0e38
EPS_LN = 1e-5
GROWS = PARTS * NE
TWO_ONES = float(np.array([0x3F803F80], np.uint32).view(np.float32)[0])
STORES = PARTS * PARTS + PARTS
LOADS = 1 + PARTS


def build(nc, x, wqT, wkT, wvT, gateT, e_bias, upT, down, shared_upT, shared_down, rope, ident_d,
          expert_rows, out):
    ctx = ExitStack()
    with ctx:
        def sb(name, shape, dt=F32):
            return ctx.enter_context(nc.sbuf_tensor(name, shape, dt))

        def sem(name):
            return ctx.enter_context(nc.semaphore(name))

        q_dram = nc.dram_tensor("q_stack", (H, PARTS, PARTS, HD, B * T), BF16).ap()
        k_dram = nc.dram_tensor("k_stack", (H, PARTS, HD, B * T), BF16).ap()

        xnT = sb("xnT", [P, B * T])
        xcur = sb("xcur", [P, T])
        wq = sb("wq", [P, D]); wk = sb("wk", [P, D]); wv = sb("wv", [P, D])
        gate = sb("gate", [P, NE]); ebias = sb("ebias", [P, NE])
        up = sb("up", [P, NE * EI]); dn = sb("dn", [P, SLICES, D])
        sup = sb("sup", [P, SI]); sdn = sb("sdn", [P, NSH, D])
        fac = sb("fac", [P, 2 * B])
        ident = sb("ident", [P, P]); identb = sb("identb", [P, P], BF16)
        exp_rows = sb("exp_rows", [GROWS, NE])
        spread = sb("spread", [GROWS, NE * EI], BF16)
        stats = sb("stats", [P, NT, 6]); mv = sb("mv", [P, NT, 2])
        ln = sb("ln", [P, 4, NT])
        qk32 = sb("qk32", [P, 2, B * T])
        qk_res = sb("qk_res", [P, 2, 2, T])
        qk_parts = sb("qk_parts", [P, 2, PARTS, T], BF16)
        stacks = sb("stacks", [P, NQ, 2, QUAD, T], BF16)
        q_st = [stacks[:, j, 0] for j in range(NQ)]
        k_st = [stacks[:, j, 1] for j in range(NQ)]
        x_in = stacks[:, NQ - 2:].rearrange("p j w h t -> p (j w h t)").bitcast(F32).rearrange(
            "p (n d) -> p n d", d=D)
        x_res = sb("x_res", [P, TT, D])
        v_aug = sb("v_aug", [P, TT, H, VW])
        probs = sb("probs", [P, 2, QUAD, T])
        ffn = sb("ffn", [P, 12, T])
        relu = ffn[:, 0:4]
        gated = ffn[:, 4:6]
        g = ffn[:, 6:8]
        sh_r, sh_g = ffn[:, 8:10], ffn[:, 10:12]
        gparts = sb("gparts", [P, TT, PARTS, NE], BF16)
        gT = sb("gT", [GROWS, T], BF16)
        att_sb = sb("att_sb", [P, T])
        rec = sb("rec", [P, TT * QUAD])
        att_y = sb("att_y", [P, TT, NQ, QUAD * HD])
        y = sb("y", [P, 2, T])
        nmax = sb("nmax", [P, TT, QUAD]); nres = sb("nres", [P, 2, TT, QUAD])
        nparts = sb("nparts", [P, TT, PARTS, QUAD], BF16)
        mrow = sb("mrow", [PARTS * QUAD, T], BF16)
        xn = probs[:].rearrange("p a h t -> p (a h t)").rearrange("p (t d) -> p t d", d=D)
        sig = sb("sig", [P, NT, NE])
        sc = sb("sc", [P, TT, NE]); tmp = sb("tmp", [P, TT, NE])
        pair = sb("pair", [P, 6, TT, NG])
        gsc = sb("gsc", [P, TT, NG + TOPG]); gtop = sb("gtop", [P, TT, 8])
        gmark = sb("gmark", [P, TT, NG + TOPG])
        msk = sb("msk", [P, TT, NE + 2]); etop = sb("etop", [P, TT, 8]); emark = sb("emark", [P, TT, NE + 2])
        wsum = sb("wsum", [P, 2, TT])

        bank = [ctx.enter_context(nc.psum_tensor(n, [P, 512], F32))
                for n in ("sc0", "sc1", "st0", "st1", "pv", "upb", "tr", "acc")]
        qk_b = (bank[4], bank[7])
        sc_b, st_b, pv_b, up_b, tr_b, acc_b = bank[0:2], bank[2:4], bank[4], bank[5], bank[6], bank[7]

        pool_waited = sem("pool_waited"); dve_waited = sem("dve_waited")
        x_res_ld = sem("x_res_ld")
        x_ld = [sem(f"x_ld{i}") for i in range(B)]
        w_ld = sem("w_ld"); w2_ld = sem("w2_ld")
        set_ready = sem("set_ready")
        pool_set = sem("pool_set")
        spread_ready = sem("spread_ready")
        link = sem("link")
        var_ready = sem("var_ready"); std_ready = sem("std_ready")
        xn_ready = sem("xn_ready"); xnT_psum = sem("xnT_psum"); xnT_ready = sem("xnT_ready")
        logit_ready = sem("logit_ready"); sig_ready = sem("sig_ready")
        route_step = sem("route_step")
        gparts_ready = sem("gparts_ready"); gT_ready = sem("gT_ready")
        proj_ready = sem("proj_ready"); qk32_ready = sem("qk32_ready")
        split_step = sem("split_step"); parts_ready = sem("parts_ready"); stored = sem("stored")
        st_ld = [sem(f"st_ld{j}") for j in range(NQ)]
        s_done = sem("s_done"); s_read = sem("s_read")
        neg_step = sem("neg_step"); negmax_ready = sem("negmax_ready")
        mrow_ready = sem("mrow_ready"); mrow_ld = sem("mrow_ld")
        t_done = sem("t_done"); probs_ready = sem("probs_ready")
        pv_done = sem("pv_done"); att_ready = sem("att_ready")
        up_done = sem("up_done"); v_ready = sem("v_ready"); relu_ready = sem("relu_ready")
        gated_ready = sem("gated_ready")
        tr_done = sem("tr_done"); g_ready = sem("g_ready")
        xcur_ready = sem("xcur_ready"); sh_relu = sem("sh_relu"); sh_ready = sem("sh_ready")
        down_done = sem("down_done"); rec_ready = sem("rec_ready"); atty_ready = sem("atty_ready")
        sum_ready = sem("sum_ready"); y_ready = sem("y_ready"); y_stored = sem("y_stored")

        def score_heads(kt, slot):
            return ((2, 1, 2, 1), (1, 2, 1, 1), (2, 1, 2, 0), (0, 0, 0, 0))[kt][slot]

        def up_slot(n):
            return 2 if n < NSH else 0

        def shared_slot(n):
            return 1 if n == 0 else 0

        def up_units():
            order = [("v", 0)]
            for n in range(SLICES):
                if n < NSH:
                    order.append(("shared", n))
                order.append(("slice", n))
            return {u: n for n, u in enumerate(order)}
        UP = up_units()
        NUP = len(UP)

        def tr_units(last):
            order = [("gate", 0)]
            for n in range(SLICES):
                j, kt = n // TT, n % TT
                if kt == TT - 1 and not (last and j == NQ - 1):
                    order.append(("max", j))
                order.append(("slice", n))
                if kt == 1 and j:
                    order.append(("att", j - 1))
            order.append(("att", NQ - 1))
            return {u: n for n, u in enumerate(order)}
        NTR = len(tr_units(False))

        def tr_count(b, last, kind, n):
            return 1 + b * NTR + tr_units(last)[kind, n] + 1

        NDOWN = SLICES + NSH

        def wait(eng, semaphore, count):
            if not isinstance(count, int) or count > 0:
                eng.wait_ge(semaphore, count)

        def over_batches(eng, body):
            body(0, 2)
            with eng.Fori(1, B - 2) as b:
                body(b, 2)
            body(B - 2, 1)
            body(B - 1, 0)

        FIRST = (slice(0, TT), slice(TT, NT))
        NW1 = 7
        ROUTE_AT = (0, 2, 5, 7, 9, 11, 13, 15, 18, 21, 25)
        ROUTE_PIECES, ROUTE_STEPS = len(ROUTE_AT) - 1, ROUTE_AT[-1]

        block = ctx.enter_context(nc.Block())

        @block.sync
        def _(sp):
            def load_x(i):
                sp.dma_start(x_in[:, i * TT:(i + 1) * TT, :],
                             x[i * T:(i + 1) * T, :].rearrange("(t p) d -> p t d", p=P)).then_inc(x_ld[i], 16)

            load_x(0)
            for dst, src in ((ident, ident_d), (wq, wqT), (wk, wkT), (fac, rope), (exp_rows, expert_rows),
                             (gate, gateT)):
                sp.dma_start(dst[:], src).then_inc(w_ld, 16)
            sp.dma_start(ebias[:], e_bias.partition_broadcast(P)).then_inc(w_ld, 16)
            for i in range(1, B):
                load_x(i)

            def store_parts(b):
                t_at = bass.ds(b * T, T)
                sp.wait_ge(parts_ready, b * 2 + 1)
                for i in range(PARTS):
                    for r in range(PARTS):
                        sp.dma_start(q_dram[:, i, r, :, t_at], qk_parts[:, 0, i, :]).then_inc(stored, 16)
                sp.wait_ge(parts_ready, b * 2 + 2)
                for i in range(PARTS):
                    sp.dma_start(k_dram[:, i, :, t_at], qk_parts[:, 1, i, :]).then_inc(stored, 16)

            def load_stack(b, j):
                heads = slice(j * QUAD, (j + 1) * QUAD)
                t_at = bass.ds(b * T, T)
                sp.wait_ge(stored, (b + 1) * (STORES * 16))
                sp.dma_start(q_st[j][0:STACK, :, :],
                             q_dram[heads, :, :, :, t_at].rearrange("h i r d t -> (i r d) h t")
                             ).then_inc(st_ld[j], 16)
                for i in range(PARTS):
                    rows = slice(i * PARTS * HD, (i + 1) * PARTS * HD)
                    sp.dma_start(k_st[j][rows, :, :],
                                 k_dram[heads, :, :, t_at].rearrange("h r d t -> (r d) h t")
                                 ).then_inc(st_ld[j], 16)

            def load_max(step, j):
                sp.wait_ge(mrow_ready, step + 1)
                sp.dma_start(q_st[j][STACK:ROWS, :, :], mrow[:, :]).then_inc(mrow_ld, 16)

            def load_residual(b):
                sp.dma_start(x_res[:], x[bass.ds(b * T, T), :].rearrange("(t p) d -> p t d", p=P)
                             ).then_inc(x_res_ld, 16)

            store_parts(0)
            sp.wait_ge(set_ready, 1)
            load_stack(0, 0)
            load_stack(0, 1)
            sp.dma_start(wv[:], wvT).then_inc(w2_ld, 16)
            sp.dma_start(sup[:], shared_upT).then_inc(w2_ld, 16)
            sp.dma_start(up[:], upT).then_inc(w2_ld, 16)
            sp.dma_start(sdn[:], shared_down.rearrange("(n p) d -> p n d", p=P)).then_inc(w2_ld, 16)
            sp.dma_start(dn[:], down.rearrange("(n p) d -> p n d", p=P)).then_inc(w2_ld, 16)
            sp.wait_ge(set_ready, 3)
            load_stack(0, 2)
            load_stack(0, 3)
            load_residual(0)
            load_max(0, 0)
            store_parts(1)

            def batch(b, more):
                for j in range(NQ):
                    if more or j < NQ - 1:
                        load_max(b * NQ + j + 1, (j + 1) % NQ)
                    if more:
                        sp.wait_ge(t_done, (b * NQ + j + 1) * TT * QUAD)
                        load_stack(b + 1, j)
                    if more == 2 and j == NQ - 2:
                        store_parts(b + 2)
                sp.wait_ge(y_ready, b + 1)
                sp.dma_start(out[bass.ds(b * T, T), :].rearrange("(t p) d -> p t d", p=P),
                             y[:, 1, :].rearrange("p (t d) -> p t d", d=D)).then_inc(y_stored, 16)
                if more:
                    load_residual(b + 1)
            over_batches(sp, batch)
            sp.wait_ge(y_stored, B * 16)

        @block.gpsimd
        def _(pool):
            def plain():
                nc.gpsimd.sem_inc(pool_waited, 1)

            nc.gpsimd.memset(k_st[0][64:96, :, :].bitcast(F32), TWO_ONES).then_inc(pool_set, 1)
            pool.wait_ge(pool_set, 1)
            nc.gpsimd.memset(k_st[1][64:96, :, :].bitcast(F32), TWO_ONES).then_inc(set_ready, 1)
            pool.wait_ge(set_ready, 1)
            nc.gpsimd.memset(v_aug[:], 0.0).then_inc(pool_set, 1)
            pool.wait_ge(pool_set, 2)
            nc.gpsimd.memset(v_aug[:, :, :, HD:HD + 1], 1.0).then_inc(set_ready, 1)
            pool.wait_ge(set_ready, 2)
            pool.wait_ge(xn_ready, B)
            nc.gpsimd.memset(k_st[2][64:96, :, :].bitcast(F32), TWO_ONES).then_inc(pool_set, 1)
            pool.wait_ge(pool_set, 3)
            nc.gpsimd.memset(k_st[3][64:96, :, :].bitcast(F32), TWO_ONES).then_inc(set_ready, 1)
            pool.wait_ge(set_ready, 3)

            def cut_step(b, w, k):
                src = qk32[:, w, bass.ds(b * T, T)]
                res, part = qk_res[:, w], qk_parts[:, w]
                if k == 0:
                    pool.wait_ge(qk32_ready, b * 2 + w + 1)
                    if w == 0:
                        pool.wait_ge(stored, b * (STORES * 16))
                else:
                    pool.wait_ge(split_step, (b - 1) * 8 + w * 4 + k)
                plain()
                if k == 0:
                    nc.gpsimd.tensor_copy(part[:, 0, :], src).then_inc(split_step, 1)
                elif k == 1:
                    nc.gpsimd.tensor_tensor(res[:, 0, :], src, part[:, 0, :], ALU.subtract).then_inc(split_step, 1)
                elif k == 2:
                    nc.gpsimd.tensor_copy(part[:, 1, :], res[:, 0, :]).then_inc(split_step, 1)
                elif k == 3:
                    nc.gpsimd.tensor_tensor(res[:, 1, :], res[:, 0, :], part[:, 1, :],
                                            ALU.subtract).then_inc(split_step, 1)
                else:
                    nc.gpsimd.tensor_copy(part[:, 2, :], res[:, 1, :]).then_inc(parts_ready, 1)

            for w in range(2):
                for k in range(5):
                    cut_step(1, w, k)

            def batch(b, more):
                for n in range(SLICES):
                    if n < NSH:
                        wait(pool, down_done, b * NDOWN)
                        pool.wait_ge(sh_relu, b * NSH + n + 1)
                        plain()
                        nc.gpsimd.tensor_tensor(sh_g[:, n, :], sh_r[:, n, :], sh_r[:, n, :],
                                                ALU.mult).then_inc(sh_ready, 1)
                    wait(pool, down_done, b * NDOWN + max(n - 1, 0))
                    pool.wait_ge(gated_ready, b * SLICES + n + 1)
                    plain()
                    nc.gpsimd.tensor_tensor(g[:, n % 2, :], gated[:, n % 2, :], relu[:, n % 4, :],
                                            ALU.mult).then_inc(g_ready, 1)
                    if more == 2 and 1 <= n < 11:
                        cut_step(b + 2, (n - 1) // 5, (n - 1) % 5)
                pool.wait_ge(x_res_ld, (b + 1) * 16)
                wait(pool, y_stored, b * 16)
                pool.wait_ge(sum_ready, b + 1)
                plain()
                nc.gpsimd.tensor_tensor(y[:, 1, :], y[:, 0, :], x_res[:].rearrange("p t d -> p (t d)"),
                                        ALU.add).then_inc(y_ready, 1)
            over_batches(pool, batch)

        @block.scalar
        def _(act):
            def std(i, tiles):
                act.wait_ge(var_ready, i + 1)
                nc.scalar.activation(ln[:, 1, tiles], ln[:, 0, tiles], ACT.Sqrt).then_inc(std_ready, 1)

            def rotate(i):
                for w in range(2):
                    act.wait_ge(proj_ready, i * 2 + w + 1)
                    nc.scalar.activation(qk32[:, w, i * T:(i + 1) * T], qk_b[w][:], ACT.Copy,
                                         scale=fac[:, i * 2 + w:i * 2 + w + 1]).then_inc(qk32_ready, 1)

            def router_scores(rows):
                act.wait_ge(logit_ready, rows[-1] + 1)
                tiles = slice(rows[0] * TT, (rows[-1] + 1) * TT)
                at = tiles.start % (NT // 2) * NE
                nc.scalar.activation(sig[:, tiles, :].rearrange("p t e -> p (t e)"),
                                     st_b[rows[0] // (B // 2)][:, at:at + len(rows) * TT * NE],
                                     ACT.Sigmoid).then_inc(sig_ready, 1)

            act.wait_ge(w_ld, NW1 * 16)
            std(0, FIRST[0])
            for i in range(B):
                act.wait_ge(xnT_psum, i + 1)
                nc.scalar.activation(xnT[:, i * T:(i + 1) * T], bank[5 + i % 2][:], ACT.Copy).then_inc(xnT_ready, 1)
                if i == 0:
                    rotate(0)
                    router_scores([0])
                    std(1, FIRST[1])
            router_scores(list(range(1, B // 2)))
            router_scores(list(range(B // 2, B)))
            for i in range(1, B):
                rotate(i)
            act.wait_ge(set_ready, 2)

            def max_rows(step, count):
                act.wait_ge(tr_done, count)
                wait(act, mrow_ld, step * 16)
                nc.scalar.activation(mrow[:, :], tr_b[:].bitcast(BF16)[0:PARTS * QUAD, 0:T],
                                     ACT.Copy).then_inc(mrow_ready, 1)

            max_rows(0, 1)

            def batch(b, more):
                last = more == 0

                def att_evac(j):
                    act.wait_ge(pv_done, b * SLICES + (j + 1) * TT)
                    if j:
                        act.wait_ge(tr_done, tr_count(b, last, "att", j - 1))
                    else:
                        wait(act, atty_ready, b * NQ)
                    nc.scalar.activation(att_sb[:], pv_b[:], ACT.Copy).then_inc(att_ready, 1)

                for j in range(NQ):
                    for kt in range(TT):
                        n = j * TT + kt
                        for h in range(QUAD):
                            i = b * (SLICES * QUAD) + n * QUAD + h
                            act.wait_ge(t_done, i + 1)
                            if h == 0:
                                if n >= 2:
                                    wait(act, pv_done, b * SLICES + n - 1)
                                else:
                                    wait(act, pv_done, b * SLICES)
                            nc.scalar.activation(probs[:, kt % 2, h, :], st_b[h % 2][:], ACT.Exp
                                                 ).then_inc(probs_ready, 1)
                            if n == 0 and h == 0:
                                act.wait_ge(tr_done, tr_count(b, last, "gate", 0))
                                nc.scalar.activation(gT[:, :], tr_b[:].bitcast(BF16)[0:GROWS, 0:T],
                                                     ACT.Copy).then_inc(gT_ready, 1)
                                wait(act, up_done, b * NUP + UP["v", 0] + 1)
                                nc.scalar.activation(v_aug[:, :, :, 0:HD],
                                                     up_b[:].rearrange("p (t h d) -> p t h d", t=TT, h=H),
                                                     ACT.Copy).then_inc(v_ready, 1)
                            if n < NSH and h == shared_slot(n):
                                wait(act, up_done, b * NUP + UP["shared", n] + 1)
                                wait(act, sh_ready, b * NSH)
                                nc.scalar.activation(sh_r[:, n, :], up_b[:], ACT.Relu).then_inc(sh_relu, 1)
                            if h == up_slot(n):
                                wait(act, up_done, b * NUP + UP["slice", n] + 1)
                                wait(act, g_ready, b * SLICES + n - 3)
                                nc.scalar.activation(relu[:, n % 4, :], up_b[:], ACT.Relu).then_inc(relu_ready, 1)
                            if kt == TT - 1 and h == 0 and not (last and j == NQ - 1):
                                max_rows(b * NQ + j + 1, tr_count(b, last, "max", j))
                            if kt == 0 and h == 2 and j:
                                att_evac(j - 1)
                att_evac(NQ - 1)
            over_batches(act, batch)

        @block.vector
        def _(dve):
            done = [0]

            def then(ins):
                done[0] += 1
                ins.then_inc(link, 1)
                dve.wait_ge(link, done[0])

            def stats_of(tiles):
                for t in range(tiles.start, tiles.stop):
                    if t % TT == 0:
                        dve.wait_ge(x_ld[t // TT], 16)
                    last = nc.vector.bn_stats(stats[:, t, :], x_in[:, t, :])
                then(last)
                for t in range(tiles.start, tiles.stop):
                    last = nc.vector.bn_aggr(mv[:, t, :], stats[:, t, :])
                then(last)
                nc.vector.tensor_scalar_add(ln[:, 0, tiles], mv[:, tiles, 1], EPS_LN).then_inc(var_ready, 1)

            def normalise(i, tiles):
                dve.wait_ge(std_ready, i + 1)
                l4 = [ln[:, k, tiles] for k in range(4)]
                then(nc.vector.reciprocal(l4[2], l4[1]))
                then(nc.vector.tensor_tensor(l4[3], l4[0], l4[2], ALU.mult))
                then(nc.vector.tensor_tensor(l4[2], l4[3], l4[1], ALU.add))
                then(nc.vector.tensor_scalar(l4[3], l4[2], 0.5, None, ALU.mult))
                then(nc.vector.reciprocal(l4[1], l4[3]))
                for t in range(tiles.start, tiles.stop):
                    last = nc.vector.tensor_scalar(xn[:, t, :], x_in[:, t, :], mv[:, t, 0:1], ln[:, 1, t:t + 1],
                                                   ALU.subtract, ALU.mult)
                    if t % TT == TT - 1:
                        last.then_inc(xn_ready, 1)

            nc.vector.memset(gsc[:, :, NG:], LOW)
            nc.vector.memset(msk[:, :, NE:], LOW)
            stats_of(FIRST[0])
            normalise(0, FIRST[0])
            stats_of(FIRST[1])
            for w in range(2):
                src, res, part = qk32[:, w, 0:T], qk_res[:, w], qk_parts[:, w]
                dve.wait_ge(qk32_ready, w + 1)
                then(nc.vector.tensor_copy(part[:, 0, :], src))
                then(nc.vector.tensor_tensor(res[:, 0, :], src, part[:, 0, :], ALU.subtract))
                then(nc.vector.tensor_copy(part[:, 1, :], res[:, 0, :]))
                then(nc.vector.tensor_tensor(res[:, 1, :], res[:, 0, :], part[:, 1, :], ALU.subtract))
                nc.vector.tensor_copy(part[:, 2, :], res[:, 1, :]).then_inc(parts_ready, 1)
            normalise(1, FIRST[1])
            dve.wait_ge(xnT_ready, 1)
            nc.vector.tensor_copy(xcur[:], xnT[:, 0:T]).then_inc(xcur_ready, 1)
            dve.wait_ge(w_ld, NW1 * 16)
            nc.vector.tensor_copy(identb[:], ident[:])
            nc.vector.tensor_copy(spread[:].rearrange("r (e i) -> r e i", i=EI),
                                  exp_rows[:].unsqueeze(2).to_broadcast([GROWS, NE, EI])).then_inc(spread_ready, 1)

            def route(b, piece):
                count = [ROUTE_AT[piece]]
                if piece in (2, 3, 5, 6):
                    nc.vector.sem_inc(dve_waited, 1)

                def then(ins):
                    count[0] += 1
                    ins.then_inc(route_step, 1)
                    dve.wait_ge(route_step, b * ROUTE_STEPS + count[0])

                tiles = bass.ds(b * TT, TT)
                e4 = sc[:].rearrange("p t (g e) -> p t g e", e=GE)
                pr = lambda n: pair[:, n, :, :]
                if piece == 0:
                    dve.wait_ge(sig_ready, 1 if isinstance(b, int) and b == 0 else 3)
                    then(nc.vector.tensor_tensor(sc[:], sig[:, tiles, :],
                                                 ebias[:, :].unsqueeze(1).to_broadcast([P, TT, NE]), ALU.add))
                    nc.vector.tensor_tensor(pr(0), e4[:, :, :, 0], e4[:, :, :, 1], ALU.max)
                    nc.vector.tensor_tensor(pr(1), e4[:, :, :, 0], e4[:, :, :, 1], ALU.min)
                    nc.vector.tensor_tensor(pr(2), e4[:, :, :, 2], e4[:, :, :, 3], ALU.max)
                    then(nc.vector.tensor_tensor(pr(3), e4[:, :, :, 2], e4[:, :, :, 3], ALU.min))
                elif piece == 1:
                    nc.vector.tensor_tensor(pr(4), pr(0), pr(2), ALU.min)
                    then(nc.vector.tensor_tensor(pr(5), pr(1), pr(3), ALU.max))
                    nc.vector.tensor_tensor(pr(1), pr(0), pr(2), ALU.max)
                    then(nc.vector.tensor_tensor(pr(3), pr(4), pr(5), ALU.max))
                    then(nc.vector.tensor_tensor(gsc[:, :, 0:NG], pr(1), pr(3), ALU.add))
                elif piece == 2:
                    for t in range(TT):
                        last = nc.vector.max(out=gtop[:, t, :], in_=gsc[:, t, 0:NG])
                    then(last)
                    then(nc.vector.memset(gtop[:, :, TOPG:], LOW))
                elif piece == 3:
                    for t in range(TT):
                        last = nc.vector.match_replace(out=gmark[:, t, :], in_to_replace=gtop[:, t, :],
                                                       in_values=gsc[:, t, :], imm_value=MARK)
                    then(last)
                    then(nc.vector.tensor_scalar(pr(0), gmark[:, :, 0:NG], MARK, None, ALU.is_equal))
                elif piece == 4:
                    then(nc.vector.tensor_tensor(tmp[:].rearrange("p t (g e) -> p t g e", e=GE), e4,
                                                 pr(0).unsqueeze(3).to_broadcast([P, TT, NG, GE]), ALU.mult))
                    then(nc.vector.tensor_scalar_add(msk[:, :, 0:NE], tmp[:], 0.0))
                elif piece == 5:
                    for t in range(TT):
                        last = nc.vector.max(out=etop[:, t, :], in_=msk[:, t, 0:NE])
                    then(last)
                    then(nc.vector.memset(etop[:, :, TOPK:], LOW))
                elif piece == 6:
                    for t in range(TT):
                        last = nc.vector.match_replace(out=emark[:, t, :], in_to_replace=etop[:, t, :],
                                                       in_values=msk[:, t, :], imm_value=MARK)
                    then(last)
                    then(nc.vector.tensor_scalar(sc[:], emark[:, :, 0:NE], MARK, None, ALU.is_equal))
                elif piece == 7:
                    then(nc.vector.tensor_tensor(tmp[:], sc[:], sig[:, tiles, :], ALU.mult))
                    then(nc.vector.tensor_reduce(out=wsum[:, 0, :], in_=tmp[:], op=ALU.add, axis=AXX))
                    then(nc.vector.tensor_scalar_add(wsum[:, 1, :], wsum[:, 0, :], 1e-20))
                elif piece == 8:
                    then(nc.vector.reciprocal(wsum[:, 0, :], wsum[:, 1, :]))
                    then(nc.vector.tensor_scalar(wsum[:, 1, :], wsum[:, 0, :], ROUTED_SCALE, None, ALU.mult))
                    then(nc.vector.tensor_tensor(tmp[:], tmp[:],
                                                 wsum[:, 1, :].unsqueeze(2).to_broadcast([P, TT, NE]), ALU.mult))
                elif piece == 9:
                    then(nc.vector.tensor_copy(gparts[:, :, 0, :], tmp[:]))
                    then(nc.vector.tensor_tensor(sc[:], tmp[:], gparts[:, :, 0, :], ALU.subtract))
                    then(nc.vector.tensor_copy(gparts[:, :, 1, :], sc[:]))
                    then(nc.vector.tensor_tensor(tmp[:], sc[:], gparts[:, :, 1, :], ALU.subtract))
                    nc.vector.tensor_copy(gparts[:, :, 2, :], tmp[:]).then_inc(gparts_ready, 1)
                assert count[0] == ROUTE_AT[piece + 1]

            for piece in range(ROUTE_PIECES):
                route(0, piece)

            def row_max(step, i):
                dve.wait_ge(s_done, step * (TT * QUAD) + i + 1)
                nc.vector.tensor_reduce(out=nmax[:, i % TT, i // TT:i // TT + 1], in_=sc_b[i % 2][:],
                                        op=ALU.max, axis=AXX, negate=True).then_inc(s_read, 1)

            def cut_max(step):
                dve.wait_ge(s_read, (step + 1) * TT * QUAD)
                nc.vector.tensor_copy(nparts[:, :, 0, :], nmax[:]).then_inc(neg_step, 1)
                dve.wait_ge(neg_step, step * 4 + 1)
                nc.vector.tensor_tensor(nres[:, 0], nmax[:], nparts[:, :, 0, :], ALU.subtract).then_inc(neg_step, 1)
                dve.wait_ge(neg_step, step * 4 + 2)
                nc.vector.tensor_copy(nparts[:, :, 1, :], nres[:, 0]).then_inc(neg_step, 1)
                dve.wait_ge(neg_step, step * 4 + 3)
                nc.vector.tensor_tensor(nres[:, 1], nres[:, 0], nparts[:, :, 1, :], ALU.subtract).then_inc(neg_step, 1)
                dve.wait_ge(neg_step, step * 4 + 4)
                nc.vector.tensor_copy(nparts[:, :, 2, :], nres[:, 1]).then_inc(negmax_ready, 1)

            for i in range(TT * QUAD):
                row_max(0, i)
            cut_max(0)

            def batch(b, more):
                last = more == 0

                def att_out(j):
                    dve.wait_ge(tr_done, tr_count(b, last, "att", j))
                    a4 = tr_b[:].rearrange("p (n c) -> p n c", c=VW)
                    nc.vector.reciprocal(rec[:].unsqueeze(2), a4[:, :, HD:HD + 1]).then_inc(rec_ready, 1)
                    wait(dve, rec_ready, b * NQ + j + 1)
                    nc.vector.tensor_tensor(att_y[:, :, j, :].rearrange("p t (h d) -> p t h d", d=HD),
                                            a4[:, :, 0:HD].rearrange("p (t h) d -> p t h d", h=QUAD),
                                            rec[:].rearrange("p (t h) -> p t h", h=QUAD).unsqueeze(3)
                                            .to_broadcast([P, TT, QUAD, HD]), ALU.mult).then_inc(atty_ready, 1)

                for j in range(NQ):
                    step = b * NQ + j + 1
                    skip = last and j == NQ - 1
                    i = 0
                    for kt in range(TT):
                        n = j * TT + kt
                        for slot in range(QUAD):
                            if kt == TT - 1 and slot == 0 and not skip:
                                cut_max(step)
                            if not skip:
                                for _ in range(score_heads(kt, slot)):
                                    row_max(step, i)
                                    i += 1
                            if slot == up_slot(n) + 1:
                                wait(dve, relu_ready, b * SLICES + n + 1)
                                dve.wait_ge(tr_done, tr_count(b, last, "slice", n))
                                wait(dve, g_ready, b * SLICES + n - 1)
                                nc.vector.tensor_tensor(gated[:, n % 2, :], tr_b[:], relu[:, n % 4, :],
                                                        ALU.mult).then_inc(gated_ready, 1)
                            if slot == 3 and kt == 1 and j:
                                att_out(j - 1)
                            if slot and kt == TT - 1 and more:
                                piece = j * (QUAD - 1) + slot - 1
                                if piece < ROUTE_PIECES:
                                    route(b + 1, piece)
                if more:
                    dve.wait_ge(up_done, (b + 1) * NUP)
                    nc.vector.tensor_copy(xcur[:], xnT[:, bass.ds((b + 1) * T, T)]).then_inc(xcur_ready, 1)
                att_out(NQ - 1)
                wait(dve, down_done, (b + 1) * NDOWN)
                wait(dve, y_ready, b)
                wait(dve, atty_ready, (b + 1) * NQ)
                nc.vector.tensor_tensor(y[:, 0, :], acc_b[:], att_y[:].rearrange("p t j c -> p (t j c)"),
                                        ALU.add).then_inc(sum_ready, 1)
            over_batches(dve, batch)

        @block.tensor
        def _(pe):
            def transpose_x(i):
                pe.wait_ge(xn_ready, i + 1)
                if i >= 2:
                    pe.wait_ge(xnT_ready, i - 1)
                for t in range(TT):
                    last = nc.tensor.transpose(bank[5 + i % 2][:, t * P:(t + 1) * P], xn[:, i * TT + t, :], ident[:])
                last.then_inc(xnT_psum, 1)

            def project(i, w):
                if i:
                    pe.wait_ge(qk32_ready, i * 2 - 1 + w)
                nc.tensor.matmul(qk_b[w][:], (wq, wk)[w][:], xnT[:, i * T:(i + 1) * T],
                                 start=True, stop=True).then_inc(proj_ready, 1)

            def logits(i):
                pe.wait_ge(xnT_ready, i + 1)
                for t in range(i * TT, (i + 1) * TT):
                    at = t % (NT // 2) * NE
                    last = nc.tensor.matmul(st_b[t // (NT // 2)][:, at:at + NE], xnT[:, t * P:(t + 1) * P],
                                            gate[:], start=True, stop=True)
                last.then_inc(logit_ready, 1)

            pe.wait_ge(w_ld, NW1 * 16)
            transpose_x(0)
            pe.wait_ge(xnT_ready, 1)
            project(0, 0)
            project(0, 1)
            logits(0)
            pe.wait_ge(sig_ready, 1)
            transpose_x(1)
            for i in range(1, B):
                if i + 1 < B:
                    transpose_x(i + 1)
                logits(i)

            def score(step, j, i):
                h, qt = i // TT, i % TT
                nc.tensor.matmul(sc_b[i % 2][:], q_st[j][0:STACK, h, qt * P:(qt + 1) * P], k_st[j][0:STACK, h, :],
                                 start=True, stop=True).then_inc(s_done, 1)

            def max_transpose(step):
                pe.wait_ge(negmax_ready, step + 1)
                for qt in range(TT):
                    last = nc.tensor.transpose(tr_b[:].bitcast(BF16)[0:PARTS * QUAD, qt * P:(qt + 1) * P],
                                               nparts[:, qt, :, :].rearrange("p i h -> p (i h)"), identb[:])
                last.then_inc(tr_done, 1)

            for i in range(TT * QUAD):
                if i < 2 * (B - 1):
                    project(i // 2 + 1, i % 2)
                if i == 0:
                    pe.wait_ge(st_ld[0], LOADS * 16)
                if i >= 2:
                    pe.wait_ge(s_read, i - 1)
                score(0, 0, i)
            max_transpose(0)
            pe.wait_ge(w2_ld, 5 * 16)
            pe.wait_ge(spread_ready, 1)
            pe.wait_ge(qk32_ready, 2 * B)
            pe.wait_ge(sig_ready, 3)

            def batch(b, more):
                last = more == 0

                def read_before(eng_unit):
                    kind, n = eng_unit
                    if kind == "v":
                        wait(pe, v_ready, b + 1)
                    elif kind == "shared":
                        wait(pe, sh_relu, b * NSH + n + 1)
                    elif kind == "up":
                        wait(pe, relu_ready, b * SLICES + n + 1)
                    elif kind == "gate":
                        pe.wait_ge(gT_ready, b + 1)
                    elif kind == "spread":
                        wait(pe, gated_ready, b * SLICES + n + 1)
                    elif kind == "max":
                        wait(pe, mrow_ready, b * NQ + n + 2)
                    elif kind == "att":
                        wait(pe, atty_ready, b * NQ + n + 1)

                def pv(n):
                    j, kt = n // TT, n % TT
                    wait(pe, probs_ready, (b * SLICES + n + 1) * QUAD)
                    if kt == 0:
                        wait(pe, att_ready, b * NQ + j)
                    for h in range(QUAD):
                        m = nc.tensor.matmul(pv_b[h * VW:(h + 1) * VW, :], v_aug[:, kt, j * QUAD + h, :],
                                             probs[:, kt % 2, h, :], start=kt == 0, stop=kt == TT - 1)
                    m.then_inc(pv_done, 1)

                def down_slice(src, weights, first, end):
                    for t in range(TT):
                        m = nc.tensor.matmul(acc_b[:, t * P:(t + 1) * P], src[:, t * P:(t + 1) * P], weights,
                                             start=first and t == 0, stop=end, skip_group_check=True)
                    m.then_inc(down_done, 1)

                def down(n):
                    wait(pe, g_ready, b * SLICES + n + 1)
                    if n == 0:
                        pe.wait_ge(sum_ready, b)
                    down_slice(g[:, n % 2, :], dn[:, n, :], n == 0, n == SLICES - 1)

                def down_shared(i):
                    wait(pe, sh_ready, b * NSH + i + 1)
                    down_slice(sh_g[:, i, :], sdn[:, i, :], False, False)

                def att_transpose(j):
                    wait(pe, att_ready, b * NQ + j + 1)
                    for t in range(TT):
                        m = nc.tensor.transpose(tr_b[:, t * P:(t + 1) * P], att_sb[:, t * P:(t + 1) * P], ident[:])
                    m.then_inc(tr_done, 1)

                tr_user = None
                for j in range(NQ):
                    step = b * NQ + j + 1
                    nxt = (j + 1) % NQ
                    skip = last and j == NQ - 1
                    i = 0
                    for kt in range(TT):
                        n = j * TT + kt
                        for h in range(QUAD):
                            at = n * QUAD + h
                            if kt == 0 and h == 0:
                                wait(pe, mrow_ld, (b * NQ + j + 1) * 16)
                            wait(pe, probs_ready, b * (SLICES * QUAD) + (at - 1 if at >= 2 else 0))
                            nc.tensor.matmul(st_b[h % 2][:], k_st[j][0:ROWS, h, kt * P:(kt + 1) * P],
                                             q_st[j][0:ROWS, h, :], start=True, stop=True).then_inc(t_done, 1)
                            if not skip and score_heads(kt, h):
                                if i == 0:
                                    pe.wait_ge(st_ld[nxt], (b + (2 if nxt == 0 else 1)) * (LOADS * 16))
                                pe.wait_ge(s_read, step * (TT * QUAD) + i - 1)
                                score(step, nxt, i)
                                i += 1
                            if n == 0 and h == 0:
                                pe.wait_ge(gparts_ready, b + 1)
                                wait(pe, atty_ready, b * NQ)
                                pe.wait_ge(mrow_ready, 1)
                                for t in range(TT):
                                    m = nc.tensor.transpose(tr_b[:].bitcast(BF16)[0:GROWS, t * P:(t + 1) * P],
                                                            gparts[:, t, :, :].rearrange("p i e -> p (i e)"),
                                                            identb[:])
                                m.then_inc(tr_done, 1)
                                tr_user = ("gate", 0)
                                pe.wait_ge(xcur_ready, b + 1)
                                wait(pe, relu_ready, b * SLICES)
                                for t in range(TT):
                                    m = nc.tensor.matmul(up_b[:, t * P:(t + 1) * P], xcur[:, t * P:(t + 1) * P],
                                                         wv[:], start=True, stop=True)
                                m.then_inc(up_done, 1)
                            if n < NSH and h == shared_slot(n):
                                read_before(("v", 0) if n == 0 else ("up", n - 1))
                                nc.tensor.matmul(up_b[:], sup[:, n * P:(n + 1) * P], xcur[:],
                                                 start=True, stop=True).then_inc(up_done, 1)
                            if h == up_slot(n):
                                read_before(("shared", n) if n < NSH else ("up", n - 1))
                                nc.tensor.matmul(up_b[:], up[:, n * P:(n + 1) * P], xcur[:],
                                                 start=True, stop=True).then_inc(up_done, 1)
                            if kt == TT - 1 and h == 0 and not skip:
                                read_before(tr_user)
                                max_transpose(step)
                                tr_user = ("max", j)
                            if h == 1 and n:
                                pv(n - 1)
                            if h == up_slot(n) + 1:
                                read_before(tr_user)
                                nc.tensor.matmul(tr_b[:], spread[:, n * P:(n + 1) * P], gT[:, :],
                                                 start=True, stop=True).then_inc(tr_done, 1)
                                tr_user = ("spread", n)
                            if h == 2 and n:
                                down(n - 1)
                            if h == 3 and kt == 1 and j:
                                read_before(tr_user)
                                att_transpose(j - 1)
                                tr_user = ("att", j - 1)
                            if not skip and score_heads(kt, h) == 2:
                                pe.wait_ge(s_read, step * (TT * QUAD) + i - 1)
                                score(step, nxt, i)
                                i += 1
                down_shared(0)
                pv(SLICES - 1)
                down_shared(1)
                down(SLICES - 1)
                read_before(tr_user)
                att_transpose(NQ - 1)
            over_batches(pe, batch)


def kernel(L0_attn_x, L0_attn_Wq, L0_attn_Wk, L0_attn_Wv, L0_ffn_gate_w, L0_ffn_e_bias, L0_ffn_up_w,
           L0_ffn_down_w, L0_ffn_shared_up_w, L0_ffn_shared_down_w):
    from concourse import bacc
    from concourse.bass_utils import run_bass_kernel_spmd

    half = HD // 2
    theta = 1.0 / 10000.0 ** (np.arange(0, HD, 2, dtype=np.float64) / HD)
    angle = np.arange(B, dtype=np.float64)[:, None] * theta[None, :]
    turn = np.concatenate([np.cos(angle) + np.sin(angle), np.cos(angle) - np.sin(angle)], axis=1)
    assert turn.shape == (B, 2 * half)
    rope = np.tile(np.stack([turn / np.sqrt(HD), turn], axis=1).reshape(2 * B, HD).T, (H, 1)).astype(np.float32)

    def lay(a):
        return np.ascontiguousarray(a)

    x = np.asarray(L0_attn_x)
    arrays = {
        "x": lay(x.reshape(B * T, D)),
        "wqT": lay(np.asarray(L0_attn_Wq).T),
        "wkT": lay(np.asarray(L0_attn_Wk).T),
        "wvT": lay(np.asarray(L0_attn_Wv).T),
        "gateT": lay(np.asarray(L0_ffn_gate_w).T),
        "e_bias": lay(np.asarray(L0_ffn_e_bias)),
        "upT": lay(np.asarray(L0_ffn_up_w).reshape(NE * EI, D).T),
        "down": lay(np.asarray(L0_ffn_down_w).transpose(0, 2, 1).reshape(NE * EI, D)),
        "shared_upT": lay(np.asarray(L0_ffn_shared_up_w).T),
        "shared_down": lay(np.asarray(L0_ffn_shared_down_w).T),
        "rope": lay(rope),
        "ident_d": np.eye(P, dtype=np.float32),
        "expert_rows": np.tile(np.eye(NE, dtype=np.float32), (PARTS, 1)),
    }
    nc = bacc.Bacc("TRN2", target_bir_lowering=False, num_devices=1)
    args = [nc.dram_tensor(f"in_{n}", a.shape, mybir.dt.from_np(a.dtype), kind="ExternalInput").ap()
            for n, a in arrays.items()]
    out = nc.dram_tensor("out", (B * T, D), F32, kind="ExternalOutput").ap()
    build(nc, *args, out)
    r = run_bass_kernel_spmd(nc, [{f"in_{n}": a for n, a in arrays.items()}], core_ids=[0])
    return r.results[0]["out"].reshape(B, T, D)
```

```python
from contextlib import ExitStack

import concourse.bass as bass
import numpy as np
from concourse import mybir

F32 = mybir.dt.float32
BF16 = mybir.dt.bfloat16
ALU = mybir.AluOpType
ACT = mybir.ActivationFunctionType
AXX = mybir.AxisListType.X

P = 128
B, T, D = 8, 512, 128
TT = T // P
NT = B * TT
H, HD = 16, 8
QUAD = 4
NQ = H // QUAD
NE, EI = 32, 64
SI = 256
NG, GE = 8, 4
TOPG, TOPK = 4, 6
ROUTED_SCALE = 2.5
SLICES = NE * EI // P
EPS = P // EI
NSH = SI // P
PARTS = 3
STACK = PARTS * PARTS * HD
MAX_AT = 96
MAX_ROWS = PARTS * QUAD
ROWS = MAX_AT + MAX_ROWS
VW = 32
LOW, MARK = -3.0e38, 3.0e38
EPS_LN = 1e-5
GROWS = PARTS * NE
TWO_ONES = np.array([0x3F803F80], np.uint32).view(np.float32)[0]
STORES = PARTS * PARTS + PARTS
LOADS = 1 + PARTS


def build(nc, x, wqT, wkT, wvT, gateT, e_bias, upT, down, shared_upT, shared_down, rope, ident_d,
          expert_rows, head_rows, out):
    ctx = ExitStack()
    with ctx:
        def sb(name, shape, dt=F32):
            return ctx.enter_context(nc.sbuf_tensor(name, shape, dt))

        def sem(name):
            return ctx.enter_context(nc.semaphore(name))

        q_dram = nc.dram_tensor("q_stack", (H, PARTS, PARTS, HD, B * T), BF16).ap()
        k_dram = nc.dram_tensor("k_stack", (H, PARTS, HD, B * T), BF16).ap()

        xnT = sb("xnT", [P, B * T])
        xcur = sb("xcur", [P, T])
        wq = sb("wq", [P, D]); wk = sb("wk", [P, D]); wv = sb("wv", [P, D])
        gate = sb("gate", [P, NE]); ebias = sb("ebias", [P, NE])
        up = sb("up", [P, NE * EI]); dn = sb("dn", [P, SLICES, D])
        sup = sb("sup", [P, SI]); sdn = sb("sdn", [P, NSH, D])
        fac = sb("fac", [P, 2 * B])
        ident = sb("ident", [P, P]); identb = sb("identb", [P, P], BF16)
        exp_rows = sb("exp_rows", [GROWS, NE])
        spread = sb("spread", [GROWS, NE * EI], BF16)
        stats = sb("stats", [P, NT, 6]); mv = sb("mv", [P, NT, 2])
        ln = sb("ln", [P, 4, NT])
        qk32 = sb("qk32", [P, 2, B * T])
        qk_res = sb("qk_res", [P, 2, 2, T])
        qk_parts = sb("qk_parts", [P, 2, PARTS, T], BF16)
        stacks = sb("stacks", [P, NQ, 2, QUAD, T], BF16)
        q_st = [stacks[:, j, 0] for j in range(NQ)]
        k_st = [stacks[:, j, 1] for j in range(NQ)]
        x_in = stacks[:, NQ - 2:].rearrange("p j w h t -> p (j w h t)").bitcast(F32).rearrange(
            "p (n d) -> p n d", d=D)
        x_res = sb("x_res", [P, TT, D])
        v_aug = sb("v_aug", [P, TT, H, VW])
        probs = sb("probs", [P, 2, QUAD, T])
        ffn = sb("ffn", [P, 12, T])
        relu = ffn[:, 0:4]
        gated = ffn[:, 4:6]
        g = ffn[:, 6:8]
        sh_r, sh_g = ffn[:, 8:10], ffn[:, 10:12]
        gparts = sb("gparts", [P, TT, PARTS, NE], BF16)
        gT = sb("gT", [GROWS, T], BF16)
        att_sb = sb("att_sb", [P, T])
        rec = sb("rec", [P, TT * QUAD])
        att_y = sb("att_y", [P, TT, NQ, QUAD * HD])
        y = sb("y", [P, 2, T])
        nmax = sb("nmax", [P, TT, QUAD]); nres = sb("nres", [P, 2, TT, QUAD])
        nparts = sb("nparts", [P, TT, PARTS, QUAD], BF16)
        mrow = sb("mrow", [P, T], BF16)
        lgT = [sh_g[:, i, :] for i in range(2)]
        xn = probs[:].rearrange("p a h t -> p (a h t)").rearrange("p (t d) -> p t d", d=D)
        sig = sb("sig", [P, NT, NE])
        sc = sb("sc", [P, TT, NE]); tmp = sb("tmp", [P, TT, NE])
        pair = sb("pair", [P, 6, TT, NG])
        gsc = sb("gsc", [P, TT, NG + TOPG]); gtop = sb("gtop", [P, TT, 8])
        gmark = sb("gmark", [P, TT, NG + TOPG])
        msk = sb("msk", [P, TT, NE + 2]); etop = sb("etop", [P, TT, 8]); emark = sb("emark", [P, TT, NE + 2])
        wsum = sb("wsum", [P, 2, TT])

        bank = [ctx.enter_context(nc.psum_tensor(n, [P, 512], F32))
                for n in ("sc0", "sc1", "st0", "st1", "pv", "upb", "tr", "acc")]
        qk_b = (bank[4], bank[7])
        sc_b, st_b, pv_b, up_b, tr_b, acc_b = bank[0:2], bank[2:4], bank[4], bank[5], bank[6], bank[7]

        pool_waited = sem("pool_waited"); dve_waited = sem("dve_waited")
        x_res_ld = sem("x_res_ld")
        x_ld = [sem(f"x_ld{i}") for i in range(B)]
        w_ld = sem("w_ld"); w2_ld = sem("w2_ld")
        set_ready = sem("set_ready")
        pool_set = sem("pool_set")
        spread_ready = sem("spread_ready")
        link = sem("link")
        var_ready = sem("var_ready"); std_ready = sem("std_ready"); inv_ready = sem("inv_ready")
        xn_ready = sem("xn_ready"); xn_pool = sem("xn_pool"); xnT_psum = sem("xnT_psum"); xnT_ready = sem("xnT_ready")
        lgT_psum = sem("lgT_psum"); lgT_ready = sem("lgT_ready")
        logit_ready = sem("logit_ready"); sig_ready = sem("sig_ready")
        route_step = sem("route_step")
        gparts_ready = sem("gparts_ready"); gT_ready = sem("gT_ready")
        proj_ready = sem("proj_ready"); qk32_ready = sem("qk32_ready")
        split_step = sem("split_step"); parts_ready = sem("parts_ready"); stored = sem("stored")
        st_ld = [sem(f"st_ld{j}") for j in range(NQ)]
        s_done = sem("s_done"); s_read = sem("s_read")
        neg_step = sem("neg_step"); negmax_ready = sem("negmax_ready")
        mrow_ready = sem("mrow_ready"); max_set = sem("max_set"); mask_ld = sem("mask_ld")
        t_done = sem("t_done"); probs_ready = sem("probs_ready")
        pv_done = sem("pv_done"); att_ready = sem("att_ready")
        up_done = sem("up_done"); v_ready = sem("v_ready"); relu_ready = sem("relu_ready")
        gated_ready = sem("gated_ready")
        tr_done = sem("tr_done"); g_ready = sem("g_ready")
        xcur_ready = sem("xcur_ready"); sh_relu = sem("sh_relu"); sh_ready = sem("sh_ready")
        down_done = sem("down_done"); rec_ready = sem("rec_ready"); atty_ready = sem("atty_ready")
        sum_ready = sem("sum_ready"); y_ready = sem("y_ready"); y_stored = sem("y_stored")

        SCORE_TILES = ((1, 1, 1, 1), (1, 1, 1, 1), (1, 1, 1, 1), (1, 1, 1, 1))
        AHEAD = sum(SCORE_TILES[TT - 1])
        assert sum(sum(row) for row in SCORE_TILES) == TT * QUAD

        def score_tiles(more, j, kt, slot):
            before = sum(SCORE_TILES[kt][:slot])
            if kt == TT - 1:
                step = j + 2
            else:
                step = j + 1
                before += AHEAD + sum(sum(row) for row in SCORE_TILES[:kt])
            if not more and step >= NQ:
                return []
            return [(step, step % NQ, before + k) for k in range(SCORE_TILES[kt][slot])]

        SPREAD_SLOT = 2
        DOWN_SLOT = 3
        MAX_SLOT = 1

        UP = {u: n for n, u in enumerate([("slice", n) for n in range(SLICES)] + [("v", 0)]
                                         + [("shared", n) for n in range(NSH)])}
        NUP = len(UP)

        def up_count(b, kind, n):
            return (1 + NSH) + (b if kind == "slice" else b - 1) * NUP + UP[kind, n] + 1

        def tr_units(last):
            order = []
            for n in range(SLICES):
                j, kt = n // TT, n % TT
                if kt == TT - 1 and not (last and j == NQ - 1):
                    order.append(("max", j))
                order.append(("slice", n))
                if kt == 1 and j:
                    order.append(("att", j - 1))
            if not last:
                order.append(("gate", 0))
            order.append(("att", NQ - 1))
            return {u: n for n, u in enumerate(order)}
        NTR = len(tr_units(False))

        def tr_count(b, last, kind, n):
            return 2 + b * NTR + tr_units(last)[kind, n] + 1

        NDOWN = SLICES + NSH

        def wait(eng, semaphore, count):
            if not isinstance(count, int) or count > 0:
                eng.wait_ge(semaphore, count)

        def over_batches(eng, body):
            body(0, 2)
            with eng.Fori(1, B - 2) as b:
                body(b, 2)
            body(B - 2, 1)
            body(B - 1, 0)

        LN_GROUPS = (slice(0, TT), slice(TT, NT // 2), slice(NT // 2, NT))
        DVE_LN, POOL_LN = (0, 1, 4, 5), (2, 3, 6, 7)
        LB = P // NE
        assert B % LB == 0 and LB * NE == P
        assert (B, LB, NSH) == (8, 4, 2)
        PRELUDE = [("x", 0), ("q", 0), ("k", 0), ("x", 1), ("q", 1), ("k", 1), ("std", 2),
                   ("x", 2), ("x", 3), ("q", 2), ("k", 2), ("q", 3), ("k", 3), ("logits", 0),
                   ("logits_out", 0), ("x", 4), ("x", 5), ("q", 4), ("k", 4), ("x", 6), ("q", 5), ("k", 5),
                   ("x", 7), ("v", 0), ("q", 6), ("k", 6), ("shared", 0), ("q", 7), ("k", 7)]
        PRELUDE_END = [("logits", 1), ("logits_out", 1), ("shared", 1)]
        FIRST_SCORE = 12
        NW1 = 7
        ROUTE_AT = (0, 2, 5, 7, 9, 11, 13, 15, 18, 21, 25)
        ROUTE_PIECES, ROUTE_STEPS = len(ROUTE_AT) - 1, ROUTE_AT[-1]

        block = ctx.enter_context(nc.Block())

        @block.sync
        def _(sp):
            def load_x(i):
                sp.dma_start(x_in[:, i * TT:(i + 1) * TT, :],
                             x[i * T:(i + 1) * T, :].rearrange("(t p) d -> p t d", p=P)).then_inc(x_ld[i], 16)

            load_x(0)
            for dst, src in ((ident, ident_d), (wq, wqT), (wk, wkT), (fac, rope), (exp_rows, expert_rows),
                             (gate, gateT)):
                sp.dma_start(dst[:], src).then_inc(w_ld, 16)
            sp.dma_start(ebias[:], e_bias.partition_broadcast(P)).then_inc(w_ld, 16)
            for i in range(1, B):
                load_x(i)
            sp.dma_start(wv[:], wvT).then_inc(w2_ld, 16)
            sp.dma_start(sup[:], shared_upT).then_inc(w2_ld, 16)

            def store_parts(b):
                t_at = bass.ds(b * T, T)
                for i in range(PARTS):
                    sp.wait_ge(parts_ready, b * (2 * PARTS) + i + 1)
                    for r in range(PARTS):
                        sp.dma_start(q_dram[:, i, r, :, t_at], qk_parts[:, 0, i, :]).then_inc(stored, 16)
                for i in range(PARTS):
                    sp.wait_ge(parts_ready, b * (2 * PARTS) + PARTS + i + 1)
                    sp.dma_start(k_dram[:, i, :, t_at], qk_parts[:, 1, i, :]).then_inc(stored, 16)

            def load_stack(b, j):
                heads = slice(j * QUAD, (j + 1) * QUAD)
                t_at = bass.ds(b * T, T)
                sp.wait_ge(stored, (b + 1) * (STORES * 16))
                sp.dma_start(q_st[j][0:STACK, :, :],
                             q_dram[heads, :, :, :, t_at].rearrange("h i r d t -> (i r d) h t")
                             ).then_inc(st_ld[j], 16)
                for i in range(PARTS):
                    rows = slice(i * PARTS * HD, (i + 1) * PARTS * HD)
                    sp.dma_start(k_st[j][rows, :, :],
                                 k_dram[heads, :, :, t_at].rearrange("h r d t -> (r d) h t")
                                 ).then_inc(st_ld[j], 16)

            def load_mask(j):
                sp.dma_start(k_st[j][MAX_AT:ROWS, :, :].rearrange("r h t -> r (h t)").bitcast(F32),
                             head_rows).then_inc(mask_ld, 16)

            def load_residual(b):
                sp.dma_start(x_res[:], x[bass.ds(b * T, T), :].rearrange("(t p) d -> p t d", p=P)
                             ).then_inc(x_res_ld, 16)

            store_parts(0)
            sp.wait_ge(set_ready, 1)
            load_stack(0, 0)
            load_stack(0, 1)
            load_mask(0)
            load_mask(1)
            sp.dma_start(up[:], upT).then_inc(w2_ld, 16)
            sp.dma_start(sdn[:], shared_down.rearrange("(n p) d -> p n d", p=P)).then_inc(w2_ld, 16)
            sp.dma_start(dn[:], down.rearrange("(n p) d -> p n d", p=P)).then_inc(w2_ld, 16)
            sp.wait_ge(set_ready, 3)
            load_stack(0, 2)
            load_stack(0, 3)
            load_mask(2)
            load_mask(3)
            load_residual(0)
            store_parts(1)

            def batch(b, more):
                for j in range(NQ):
                    if more:
                        sp.wait_ge(t_done, (b * NQ + j + 1) * TT * QUAD)
                        load_stack(b + 1, j)
                    if more == 2 and j == NQ - 2:
                        store_parts(b + 2)
                sp.wait_ge(y_ready, b + 1)
                sp.dma_start(out[bass.ds(b * T, T), :].rearrange("(t p) d -> p t d", p=P),
                             y[:, 1, :].rearrange("p (t d) -> p t d", d=D)).then_inc(y_stored, 16)
                if more:
                    load_residual(b + 1)
            over_batches(sp, batch)
            sp.wait_ge(y_stored, B * 16)

        @block.gpsimd
        def _(pool):
            def plain():
                nc.gpsimd.sem_inc(pool_waited, 1)

            def clear(quads):
                return nc.gpsimd.memset(stacks[64:MAX_AT, quads].rearrange("p j w h t -> p (j w h t)").bitcast(F32), 0.0)

            clear(slice(0, 2)).then_inc(set_ready, 1)
            pool.wait_ge(set_ready, 1)
            nc.gpsimd.memset(v_aug[:], 0.0).then_inc(pool_set, 1)
            pool.wait_ge(pool_set, 1)
            nc.gpsimd.memset(v_aug[:, :, :, HD:HD + 1], 1.0).then_inc(set_ready, 1)
            pool.wait_ge(set_ready, 2)
            pool.wait_ge(w_ld, NW1 * 16)
            nc.gpsimd.tensor_copy(identb[:], ident[:])
            nc.gpsimd.tensor_copy(spread[:].rearrange("r (e i) -> r e i", i=EI),
                                  exp_rows[:].unsqueeze(2).to_broadcast([GROWS, NE, EI])).then_inc(spread_ready, 1)
            pool.wait_ge(xnT_ready, 1)
            nc.gpsimd.tensor_copy(xcur[:], xnT[:, 0:T]).then_inc(xcur_ready, 1)
            for i in POOL_LN:
                pool.wait_ge(inv_ready, 1 if i < B // 2 else 2)
                for t in range(i * TT, (i + 1) * TT):
                    last = nc.gpsimd.tensor_scalar(xn[:, t, :], x_in[:, t, :], mv[:, t, 0:1], ln[:, 1, t:t + 1],
                                                   ALU.subtract, ALU.mult)
                last.then_inc(xn_pool, 1)
            pool.wait_ge(xn_ready, len(DVE_LN))
            pool.wait_ge(xn_pool, len(POOL_LN))
            clear(slice(2, 4)).then_inc(set_ready, 1)
            pool.wait_ge(set_ready, 3)

            def cut_step(b, w, k):
                src = qk32[:, w, bass.ds(b * T, T)]
                res, part = qk_res[:, w], qk_parts[:, w]
                if k == 0:
                    pool.wait_ge(qk32_ready, b * 2 + w + 1)
                    if w == 0:
                        pool.wait_ge(stored, b * (STORES * 16))
                elif k % 2:
                    pool.wait_ge(parts_ready, b * (2 * PARTS) + w * PARTS + k // 2 + 1)
                else:
                    pool.wait_ge(split_step, (b - 1) * 4 + w * 2 + k // 2)
                plain()
                if k == 0:
                    nc.gpsimd.tensor_copy(part[:, 0, :], src).then_inc(parts_ready, 1)
                elif k == 1:
                    nc.gpsimd.tensor_tensor(res[:, 0, :], src, part[:, 0, :], ALU.subtract).then_inc(split_step, 1)
                elif k == 2:
                    nc.gpsimd.tensor_copy(part[:, 1, :], res[:, 0, :]).then_inc(parts_ready, 1)
                elif k == 3:
                    nc.gpsimd.tensor_tensor(res[:, 1, :], res[:, 0, :], part[:, 1, :],
                                            ALU.subtract).then_inc(split_step, 1)
                else:
                    nc.gpsimd.tensor_copy(part[:, 2, :], res[:, 1, :]).then_inc(parts_ready, 1)

            for w in range(2):
                for k in range(5):
                    cut_step(1, w, k)

            def batch(b, more):
                for n in range(SLICES):
                    if n < NSH:
                        wait(pool, down_done, b * NDOWN)
                        pool.wait_ge(sh_relu, b * NSH + n + 1)
                        plain()
                        nc.gpsimd.tensor_tensor(sh_g[:, n, :], sh_r[:, n, :], sh_r[:, n, :],
                                                ALU.mult).then_inc(sh_ready, 1)
                    wait(pool, down_done, b * NDOWN + max(n - 1, 0))
                    pool.wait_ge(gated_ready, b * SLICES + n + 1)
                    plain()
                    nc.gpsimd.tensor_tensor(g[:, n % 2, :], gated[:, n % 2, :], relu[:, n % 4, :],
                                            ALU.mult).then_inc(g_ready, 1)
                    if more == 2 and 1 <= n < 11:
                        cut_step(b + 2, (n - 1) // 5, (n - 1) % 5)
                pool.wait_ge(x_res_ld, (b + 1) * 16)
                wait(pool, y_stored, b * 16)
                pool.wait_ge(sum_ready, b + 1)
                plain()
                nc.gpsimd.tensor_tensor(y[:, 1, :], y[:, 0, :], x_res[:].rearrange("p t d -> p (t d)"),
                                        ALU.add).then_inc(y_ready, 1)
            over_batches(pool, batch)

        @block.scalar
        def _(act):
            def std(i, tiles):
                act.wait_ge(var_ready, i + 1)
                nc.scalar.activation(ln[:, 1, tiles], ln[:, 0, tiles], ACT.Sqrt).then_inc(std_ready, 1)

            def rotate(i, w):
                act.wait_ge(proj_ready, i * 2 + w + 1)
                nc.scalar.activation(qk32[:, w, i * T:(i + 1) * T], qk_b[w][:], ACT.Copy,
                                     scale=fac[:, i * 2 + w:i * 2 + w + 1]).then_inc(qk32_ready, 1)

            def router_scores(i):
                act.wait_ge(logit_ready, i + 1)
                nc.scalar.activation(sig[:, i * LB * TT:(i + 1) * LB * TT, :].rearrange(
                                         "p (b t) e -> p t b e", t=TT),
                                     st_b[1][:].rearrange("p (t b e) -> p t b e", t=TT, b=LB),
                                     ACT.Sigmoid).then_inc(sig_ready, 1)

            def v_out(b):
                wait(act, pv_done, b * SLICES)
                act.wait_ge(up_done, up_count(b, "v", 0))
                nc.scalar.activation(v_aug[:, :, :, 0:HD],
                                     up_b[:].rearrange("p (t h d) -> p t h d", t=TT, h=H),
                                     ACT.Copy).then_inc(v_ready, 1)

            def shared_relu(b, n):
                act.wait_ge(up_done, up_count(b, "shared", n))
                wait(act, sh_ready, b * NSH)
                nc.scalar.activation(sh_r[:, n, :], up_b[:], ACT.Relu).then_inc(sh_relu, 1)

            std(0, LN_GROUPS[0])
            act.wait_ge(w_ld, NW1 * 16)

            def prelude(kind, i):
                if kind == "x":
                    act.wait_ge(xnT_psum, i + 1)
                    nc.scalar.activation(xnT[:, i * T:(i + 1) * T], bank[5 + i % 2][:], ACT.Copy
                                         ).then_inc(xnT_ready, 1)
                    if i == 0:
                        std(1, LN_GROUPS[1])
                elif kind in ("q", "k"):
                    rotate(i, "qk".index(kind))
                elif kind == "std":
                    std(2, LN_GROUPS[2])
                elif kind == "logits":
                    act.wait_ge(lgT_psum, i + 1)
                    nc.scalar.activation(lgT[i], st_b[0][:], ACT.Copy).then_inc(lgT_ready, 1)
                elif kind == "logits_out":
                    router_scores(i)
                elif kind == "v":
                    act.wait_ge(set_ready, 2)
                    v_out(0)
                elif kind == "shared":
                    shared_relu(0, i)

            for kind, i in PRELUDE:
                prelude(kind, i)

            def max_rows(step, count):
                act.wait_ge(tr_done, count)
                wait(act, max_set, step)
                nc.scalar.activation(mrow[MAX_AT:ROWS, :], tr_b[:].bitcast(BF16)[MAX_AT:ROWS, 0:T],
                                     ACT.Copy).then_inc(mrow_ready, 1)

            def gate_out(count):
                act.wait_ge(tr_done, count)
                nc.scalar.activation(gT[:, :], tr_b[:].bitcast(BF16)[0:GROWS, 0:T], ACT.Copy).then_inc(gT_ready, 1)

            max_rows(0, 1)
            for kind, i in PRELUDE_END:
                prelude(kind, i)
            gate_out(2)

            def batch(b, more):
                last = more == 0

                def att_evac(j):
                    act.wait_ge(pv_done, b * SLICES + (j + 1) * TT)
                    if j:
                        act.wait_ge(tr_done, tr_count(b, last, "att", j - 1))
                    else:
                        wait(act, atty_ready, b * NQ)
                    nc.scalar.activation(att_sb[:], pv_b[:], ACT.Copy).then_inc(att_ready, 1)

                for j in range(NQ):
                    for kt in range(TT):
                        n = j * TT + kt
                        for h in range(QUAD):
                            i = b * (SLICES * QUAD) + n * QUAD + h
                            act.wait_ge(t_done, i + 1)
                            if h == 0:
                                if n >= 2:
                                    wait(act, pv_done, b * SLICES + n - 1)
                                else:
                                    wait(act, pv_done, b * SLICES)
                            nc.scalar.activation(probs[:, kt % 2, h, :], st_b[h % 2][:], ACT.Exp
                                                 ).then_inc(probs_ready, 1)
                            if h == (0 if n else 1):
                                act.wait_ge(up_done, up_count(b, "slice", n))
                                wait(act, g_ready, b * SLICES + n - 3)
                                nc.scalar.activation(relu[:, n % 4, :], up_b[:], ACT.Relu).then_inc(relu_ready, 1)
                            if kt == TT - 1 and h == MAX_SLOT and not (last and j == NQ - 1):
                                max_rows(b * NQ + j + 1, tr_count(b, last, "max", j))
                            if kt == 0 and h == 2 and j:
                                att_evac(j - 1)
                if more:
                    v_out(b + 1)
                att_evac(NQ - 1)
                if more:
                    gate_out(tr_count(b, last, "gate", 0))
                    for n in range(NSH):
                        shared_relu(b + 1, n)
            over_batches(act, batch)

        @block.vector
        def _(dve):
            done = [0]

            def then(ins):
                done[0] += 1
                ins.then_inc(link, 1)
                dve.wait_ge(link, done[0])

            def stats_of(tiles):
                for t in range(tiles.start, tiles.stop):
                    if t % TT == 0:
                        dve.wait_ge(x_ld[t // TT], 16)
                    last = nc.vector.bn_stats(stats[:, t, :], x_in[:, t, :])
                then(last)
                for t in range(tiles.start, tiles.stop):
                    last = nc.vector.bn_aggr(mv[:, t, :], stats[:, t, :])
                then(last)
                nc.vector.tensor_scalar_add(ln[:, 0, tiles], mv[:, tiles, 1], EPS_LN).then_inc(var_ready, 1)

            def invert(i, tiles):
                dve.wait_ge(std_ready, i + 1)
                l4 = [ln[:, k, tiles] for k in range(4)]
                then(nc.vector.reciprocal(l4[2], l4[1]))
                then(nc.vector.tensor_tensor(l4[3], l4[0], l4[2], ALU.mult))
                then(nc.vector.tensor_tensor(l4[2], l4[3], l4[1], ALU.add))
                then(nc.vector.tensor_scalar(l4[3], l4[2], 0.5, None, ALU.mult))
                return nc.vector.reciprocal(l4[1], l4[3])

            def normalise(i):
                for t in range(i * TT, (i + 1) * TT):
                    last = nc.vector.tensor_scalar(xn[:, t, :], x_in[:, t, :], mv[:, t, 0:1], ln[:, 1, t:t + 1],
                                                   ALU.subtract, ALU.mult)
                last.then_inc(xn_ready, 1)

            nc.vector.memset(gsc[:, :, NG:], LOW)
            nc.vector.memset(msk[:, :, NE:], LOW)
            stats_of(LN_GROUPS[0])
            then(invert(0, LN_GROUPS[0]))
            normalise(0)
            stats_of(LN_GROUPS[1])
            invert(1, LN_GROUPS[1]).then_inc(inv_ready, 1)
            for w in range(2):
                src, res, part = qk32[:, w, 0:T], qk_res[:, w], qk_parts[:, w]

                def part_of(k, rest):
                    nc.vector.tensor_copy(part[:, k, :], rest).then_inc(parts_ready, 1)
                    dve.wait_ge(parts_ready, w * PARTS + k + 1)

                dve.wait_ge(qk32_ready, w + 1)
                if w == 0:
                    dve.wait_ge(inv_ready, 1)
                part_of(0, src)
                then(nc.vector.tensor_tensor(res[:, 0, :], src, part[:, 0, :], ALU.subtract))
                part_of(1, res[:, 0, :])
                then(nc.vector.tensor_tensor(res[:, 1, :], res[:, 0, :], part[:, 1, :], ALU.subtract))
                part_of(2, res[:, 1, :])
                if w == 0:
                    normalise(DVE_LN[1])
            stats_of(LN_GROUPS[2])
            invert(2, LN_GROUPS[2]).then_inc(inv_ready, 1)
            dve.wait_ge(inv_ready, 2)
            for i in DVE_LN[2:]:
                normalise(i)

            def route(b, piece):
                count = [ROUTE_AT[piece]]
                if piece in (2, 3, 5, 6):
                    nc.vector.sem_inc(dve_waited, 1)

                def then(ins):
                    count[0] += 1
                    ins.then_inc(route_step, 1)
                    dve.wait_ge(route_step, b * ROUTE_STEPS + count[0])

                tiles = bass.ds(b * TT, TT)
                e4 = sc[:].rearrange("p t (g e) -> p t g e", e=GE)
                pr = lambda n: pair[:, n, :, :]
                if piece == 0:
                    dve.wait_ge(sig_ready, 1 if isinstance(b, int) and b == 0 else B // LB)
                    then(nc.vector.tensor_tensor(sc[:], sig[:, tiles, :],
                                                 ebias[:, :].unsqueeze(1).to_broadcast([P, TT, NE]), ALU.add))
                    nc.vector.tensor_tensor(pr(0), e4[:, :, :, 0], e4[:, :, :, 1], ALU.max)
                    nc.vector.tensor_tensor(pr(1), e4[:, :, :, 0], e4[:, :, :, 1], ALU.min)
                    nc.vector.tensor_tensor(pr(2), e4[:, :, :, 2], e4[:, :, :, 3], ALU.max)
                    then(nc.vector.tensor_tensor(pr(3), e4[:, :, :, 2], e4[:, :, :, 3], ALU.min))
                elif piece == 1:
                    nc.vector.tensor_tensor(pr(4), pr(0), pr(2), ALU.min)
                    then(nc.vector.tensor_tensor(pr(5), pr(1), pr(3), ALU.max))
                    nc.vector.tensor_tensor(pr(1), pr(0), pr(2), ALU.max)
                    then(nc.vector.tensor_tensor(pr(3), pr(4), pr(5), ALU.max))
                    then(nc.vector.tensor_tensor(gsc[:, :, 0:NG], pr(1), pr(3), ALU.add))
                elif piece == 2:
                    for t in range(TT):
                        last = nc.vector.max(out=gtop[:, t, :], in_=gsc[:, t, 0:NG])
                    then(last)
                    then(nc.vector.memset(gtop[:, :, TOPG:], LOW))
                elif piece == 3:
                    for t in range(TT):
                        last = nc.vector.match_replace(out=gmark[:, t, :], in_to_replace=gtop[:, t, :],
                                                       in_values=gsc[:, t, :], imm_value=MARK)
                    then(last)
                    then(nc.vector.tensor_scalar(pr(0), gmark[:, :, 0:NG], MARK, None, ALU.is_equal))
                elif piece == 4:
                    then(nc.vector.tensor_tensor(tmp[:].rearrange("p t (g e) -> p t g e", e=GE), e4,
                                                 pr(0).unsqueeze(3).to_broadcast([P, TT, NG, GE]), ALU.mult))
                    then(nc.vector.tensor_scalar_add(msk[:, :, 0:NE], tmp[:], 0.0))
                elif piece == 5:
                    for t in range(TT):
                        last = nc.vector.max(out=etop[:, t, :], in_=msk[:, t, 0:NE])
                    then(last)
                    then(nc.vector.memset(etop[:, :, TOPK:], LOW))
                elif piece == 6:
                    for t in range(TT):
                        last = nc.vector.match_replace(out=emark[:, t, :], in_to_replace=etop[:, t, :],
                                                       in_values=msk[:, t, :], imm_value=MARK)
                    then(last)
                    then(nc.vector.tensor_scalar(sc[:], emark[:, :, 0:NE], MARK, None, ALU.is_equal))
                elif piece == 7:
                    then(nc.vector.tensor_tensor(tmp[:], sc[:], sig[:, tiles, :], ALU.mult))
                    then(nc.vector.tensor_reduce(out=wsum[:, 0, :], in_=tmp[:], op=ALU.add, axis=AXX))
                    then(nc.vector.tensor_scalar_add(wsum[:, 1, :], wsum[:, 0, :], 1e-20))
                elif piece == 8:
                    then(nc.vector.reciprocal(wsum[:, 0, :], wsum[:, 1, :]))
                    then(nc.vector.tensor_scalar(wsum[:, 1, :], wsum[:, 0, :], ROUTED_SCALE, None, ALU.mult))
                    then(nc.vector.tensor_tensor(tmp[:], tmp[:],
                                                 wsum[:, 1, :].unsqueeze(2).to_broadcast([P, TT, NE]), ALU.mult))
                elif piece == 9:
                    then(nc.vector.tensor_copy(gparts[:, :, 0, :], tmp[:]))
                    then(nc.vector.tensor_tensor(sc[:], tmp[:], gparts[:, :, 0, :], ALU.subtract))
                    then(nc.vector.tensor_copy(gparts[:, :, 1, :], sc[:]))
                    then(nc.vector.tensor_tensor(tmp[:], sc[:], gparts[:, :, 1, :], ALU.subtract))
                    nc.vector.tensor_copy(gparts[:, :, 2, :], tmp[:]).then_inc(gparts_ready, 1)
                assert count[0] == ROUTE_AT[piece + 1]

            def row_max(step, i):
                dve.wait_ge(s_done, step * (TT * QUAD) + i + 1)
                nc.vector.tensor_reduce(out=nmax[:, i % TT, i // TT:i // TT + 1], in_=sc_b[i % 2][:],
                                        op=ALU.max, axis=AXX, negate=True).then_inc(s_read, 1)

            def cut_max(step):
                dve.wait_ge(s_read, (step + 1) * TT * QUAD)
                nc.vector.tensor_copy(nparts[:, :, 0, :], nmax[:]).then_inc(neg_step, 1)
                dve.wait_ge(neg_step, step * 4 + 1)
                nc.vector.tensor_tensor(nres[:, 0], nmax[:], nparts[:, :, 0, :], ALU.subtract).then_inc(neg_step, 1)
                dve.wait_ge(neg_step, step * 4 + 2)
                nc.vector.tensor_copy(nparts[:, :, 1, :], nres[:, 0]).then_inc(neg_step, 1)
                dve.wait_ge(neg_step, step * 4 + 3)
                nc.vector.tensor_tensor(nres[:, 1], nres[:, 0], nparts[:, :, 1, :], ALU.subtract).then_inc(neg_step, 1)
                dve.wait_ge(neg_step, step * 4 + 4)
                nc.vector.tensor_copy(nparts[:, :, 2, :], nres[:, 1]).then_inc(negmax_ready, 1)

            def set_max(step, j):
                dve.wait_ge(mrow_ready, step + 1)
                nc.vector.tensor_copy(q_st[j][MAX_AT:ROWS, :, :],
                                      mrow[MAX_AT:ROWS, :].unsqueeze(1).to_broadcast([MAX_ROWS, QUAD, T])
                                      ).then_inc(max_set, 1)

            for i in range(TT * QUAD):
                row_max(0, i)
                if 3 <= i < 3 + ROUTE_PIECES:
                    route(0, i - 3)
            cut_max(0)
            for i in range(AHEAD):
                row_max(1, i)
                if i == 1:
                    dve.wait_ge(set_ready, 3)
                    set_max(0, 0)

            def batch(b, more):
                last = more == 0

                def att_out(j):
                    dve.wait_ge(tr_done, tr_count(b, last, "att", j))
                    a4 = tr_b[:].rearrange("p (n c) -> p n c", c=VW)
                    nc.vector.reciprocal(rec[:].unsqueeze(2), a4[:, :, HD:HD + 1]).then_inc(rec_ready, 1)
                    wait(dve, rec_ready, b * NQ + j + 1)
                    nc.vector.tensor_tensor(att_y[:, :, j, :].rearrange("p t (h d) -> p t h d", d=HD),
                                            a4[:, :, 0:HD].rearrange("p (t h) d -> p t h d", h=QUAD),
                                            rec[:].rearrange("p (t h) -> p t h", h=QUAD).unsqueeze(3)
                                            .to_broadcast([P, TT, QUAD, HD]), ALU.mult).then_inc(atty_ready, 1)

                for j in range(NQ):
                    step = b * NQ + j + 1
                    skip = last and j == NQ - 1
                    for kt in range(TT):
                        n = j * TT + kt
                        for slot in range(QUAD):
                            if kt == TT - 1 and slot == 0 and not skip:
                                cut_max(step)
                            for s, _, i in score_tiles(more, j, kt, slot):
                                row_max(b * NQ + s, i)
                            if kt == TT - 1 and slot == MAX_SLOT + 1 and not skip:
                                set_max(step, (j + 1) % NQ)
                            if slot == SPREAD_SLOT:
                                wait(dve, relu_ready, b * SLICES + n + 1)
                                dve.wait_ge(tr_done, tr_count(b, last, "slice", n))
                                wait(dve, g_ready, b * SLICES + n - 1)
                                nc.vector.tensor_tensor(gated[:, n % 2, :], tr_b[:], relu[:, n % 4, :],
                                                        ALU.mult).then_inc(gated_ready, 1)
                            if slot == 0 and kt == 2 and j:
                                att_out(j - 1)
                            if slot == 1 and n == SLICES - 1 and more:
                                dve.wait_ge(up_done, up_count(b, "slice", n))
                                nc.vector.tensor_copy(xcur[:], xnT[:, bass.ds((b + 1) * T, T)]
                                                      ).then_inc(xcur_ready, 1)
                            if slot == 1 and 1 <= n <= ROUTE_PIECES and more:
                                route(b + 1, n - 1)
                att_out(NQ - 1)
                wait(dve, down_done, (b + 1) * NDOWN)
                wait(dve, y_ready, b)
                wait(dve, atty_ready, (b + 1) * NQ)
                nc.vector.tensor_tensor(y[:, 0, :], acc_b[:], att_y[:].rearrange("p t j c -> p (t j c)"),
                                        ALU.add).then_inc(sum_ready, 1)
            over_batches(dve, batch)

        @block.tensor
        def _(pe):
            def transpose_x(i):
                if i in DVE_LN:
                    pe.wait_ge(xn_ready, DVE_LN.index(i) + 1)
                else:
                    pe.wait_ge(xn_pool, POOL_LN.index(i) + 1)
                if i >= 2:
                    pe.wait_ge(xnT_ready, i - 1)
                for t in range(TT):
                    last = nc.tensor.transpose(bank[5 + i % 2][:, t * P:(t + 1) * P], xn[:, i * TT + t, :], ident[:])
                last.then_inc(xnT_psum, 1)

            def project(i, w):
                if i:
                    pe.wait_ge(qk32_ready, i * 2 - 1 + w)
                nc.tensor.matmul(qk_b[w][:], (wq, wk)[w][:], xnT[:, i * T:(i + 1) * T],
                                 start=True, stop=True).then_inc(proj_ready, 1)

            def logits(i):
                pe.wait_ge(xnT_ready, (i + 1) * LB)
                if i:
                    pe.wait_ge(lgT_ready, i)
                for k in range(LB):
                    b = i * LB + k
                    m = nc.tensor.matmul(st_b[0][k * NE:(k + 1) * NE, :], gate[:], xnT[:, b * T:(b + 1) * T],
                                         start=True, stop=True)
                m.then_inc(lgT_psum, 1)

            def logits_transpose(i):
                pe.wait_ge(lgT_ready, i + 1)
                if i:
                    pe.wait_ge(sig_ready, i)
                for t in range(TT):
                    m = nc.tensor.transpose(st_b[1][:, t * P:(t + 1) * P], lgT[i][:, t * P:(t + 1) * P], ident[:])
                m.then_inc(logit_ready, 1)

            def make_v(b):
                pe.wait_ge(xcur_ready, b + 1)
                for t in range(TT):
                    m = nc.tensor.matmul(up_b[:, t * P:(t + 1) * P], xcur[:, t * P:(t + 1) * P],
                                         wv[:], start=True, stop=True)
                m.then_inc(up_done, 1)

            def gate_transpose(b):
                pe.wait_ge(gparts_ready, b + 1)
                for t in range(TT):
                    m = nc.tensor.transpose(tr_b[:].bitcast(BF16)[0:GROWS, t * P:(t + 1) * P],
                                            gparts[:, t, :, :].rearrange("p i e -> p (i e)"), identb[:])
                m.then_inc(tr_done, 1)

            def shared_up(n):
                nc.tensor.matmul(up_b[:], sup[:, n * P:(n + 1) * P], xcur[:],
                                 start=True, stop=True).then_inc(up_done, 1)

            pe.wait_ge(w_ld, NW1 * 16)

            def prelude(kind, i):
                if kind == "x":
                    transpose_x(i)
                elif kind in ("q", "k"):
                    if kind == "q":
                        pe.wait_ge(xnT_ready, i + 1)
                    project(i, "qk".index(kind))
                elif kind == "logits":
                    logits(i)
                elif kind == "logits_out":
                    logits_transpose(i)
                elif kind == "v":
                    pe.wait_ge(w2_ld, 2 * 16)
                    pe.wait_ge(xnT_ready, B - 1)
                    make_v(0)
                elif kind == "shared":
                    if i == 0:
                        pe.wait_ge(v_ready, 1)
                    else:
                        pe.wait_ge(sh_relu, i)
                    shared_up(i)

            def score(step, j, i):
                h, qt = i // TT, i % TT
                nc.tensor.matmul(sc_b[i % 2][:], q_st[j][0:STACK, h, qt * P:(qt + 1) * P], k_st[j][0:STACK, h, :],
                                 start=True, stop=True).then_inc(s_done, 1)

            def max_transpose(step):
                pe.wait_ge(negmax_ready, step + 1)
                for qt in range(TT):
                    last = nc.tensor.transpose(tr_b[:].bitcast(BF16)[MAX_AT:ROWS, qt * P:(qt + 1) * P],
                                               nparts[:, qt, :, :].rearrange("p i h -> p (i h)"), identb[:])
                last.then_inc(tr_done, 1)

            for kind, n in PRELUDE[:FIRST_SCORE]:
                prelude(kind, n)
            rest = PRELUDE[FIRST_SCORE:]
            for i in range(TT * QUAD):
                if i == 0:
                    pe.wait_ge(st_ld[0], LOADS * 16)
                if i >= 2:
                    pe.wait_ge(s_read, i - 1)
                score(0, 0, i)
                for kind, n in rest[i * len(rest) // (TT * QUAD):(i + 1) * len(rest) // (TT * QUAD)]:
                    prelude(kind, n)
            pe.wait_ge(xnT_ready, B)
            pe.wait_ge(spread_ready, 1)
            max_transpose(0)
            pe.wait_ge(st_ld[1], LOADS * 16)
            for i in range(AHEAD):
                pe.wait_ge(s_read, TT * QUAD + i - 1)
                score(1, 1, i)
                if i < len(PRELUDE_END):
                    prelude(*PRELUDE_END[i])
            pe.wait_ge(mrow_ready, 1)
            gate_transpose(0)
            pe.wait_ge(qk32_ready, 2 * B)
            pe.wait_ge(sig_ready, B // LB)
            pe.wait_ge(w2_ld, 5 * 16)
            pe.wait_ge(mask_ld, NQ * 16)

            def batch(b, more):
                last = more == 0

                def read_before(eng_unit):
                    kind, n = eng_unit
                    if kind == "up":
                        wait(pe, relu_ready, b * SLICES + n + 1)
                    elif kind == "spread":
                        wait(pe, gated_ready, b * SLICES + n + 1)
                    elif kind == "max":
                        wait(pe, mrow_ready, b * NQ + n + 2)
                    elif kind == "att":
                        wait(pe, atty_ready, b * NQ + n + 1)

                def pv(n):
                    j, kt = n // TT, n % TT
                    wait(pe, probs_ready, (b * SLICES + n + 1) * QUAD)
                    if kt == 0:
                        wait(pe, att_ready, b * NQ + j)
                    for h in range(QUAD):
                        m = nc.tensor.matmul(pv_b[h * VW:(h + 1) * VW, :], v_aug[:, kt, j * QUAD + h, :],
                                             probs[:, kt % 2, h, :], start=kt == 0, stop=kt == TT - 1)
                    m.then_inc(pv_done, 1)

                def down_slice(src, weights, first, end):
                    for t in range(TT):
                        m = nc.tensor.matmul(acc_b[:, t * P:(t + 1) * P], src[:, t * P:(t + 1) * P], weights,
                                             start=first and t == 0, stop=end, skip_group_check=True)
                    m.then_inc(down_done, 1)

                def down(n):
                    wait(pe, g_ready, b * SLICES + n + 1)
                    if n == 0:
                        pe.wait_ge(sum_ready, b)
                    down_slice(g[:, n % 2, :], dn[:, n, :], n == 0, n == SLICES - 1)

                def down_shared(i):
                    wait(pe, sh_ready, b * NSH + i + 1)
                    down_slice(sh_g[:, i, :], sdn[:, i, :], False, False)

                def att_transpose(j):
                    wait(pe, att_ready, b * NQ + j + 1)
                    for t in range(TT):
                        m = nc.tensor.transpose(tr_b[:, t * P:(t + 1) * P], att_sb[:, t * P:(t + 1) * P], ident[:])
                    m.then_inc(tr_done, 1)

                def next_score(tile):
                    s, quad, i = tile
                    if i == 0:
                        pe.wait_ge(st_ld[quad], (b + 1 + s // NQ) * (LOADS * 16))
                    pe.wait_ge(s_read, (b * NQ + s) * (TT * QUAD) + i - 1)
                    score(b * NQ + s, quad, i)

                tr_user = None
                for j in range(NQ):
                    step = b * NQ + j + 1
                    skip = last and j == NQ - 1
                    for kt in range(TT):
                        n = j * TT + kt
                        for h in range(QUAD):
                            tiles = score_tiles(more, j, kt, h)
                            at = n * QUAD + h
                            if kt == 0 and h == 0:
                                wait(pe, max_set, b * NQ + j + 1)
                            wait(pe, probs_ready, b * (SLICES * QUAD) + (at - 1 if at >= 2 else 0))
                            nc.tensor.matmul(st_b[h % 2][:], k_st[j][0:ROWS, h, kt * P:(kt + 1) * P],
                                             q_st[j][0:ROWS, h, :], start=True, stop=True).then_inc(t_done, 1)
                            if tiles:
                                next_score(tiles[0])
                            if h == (0 if n else 1):
                                if n == 0:
                                    wait(pe, sh_relu, (b + 1) * NSH)
                                else:
                                    read_before(("up", n - 1))
                                nc.tensor.matmul(up_b[:], up[:, n * P:(n + 1) * P], xcur[:],
                                                 start=True, stop=True).then_inc(up_done, 1)
                            if kt == TT - 1 and h == MAX_SLOT and not skip:
                                read_before(tr_user)
                                max_transpose(step)
                                tr_user = ("max", j)
                            if h == 1 and n:
                                pv(n - 1)
                            if h == SPREAD_SLOT:
                                if n == 0:
                                    wait(pe, atty_ready, b * NQ)
                                    pe.wait_ge(gT_ready, b + 1)
                                else:
                                    read_before(tr_user)
                                nc.tensor.matmul(tr_b[:], spread[:, n * P:(n + 1) * P], gT[:, :],
                                                 start=True, stop=True).then_inc(tr_done, 1)
                                tr_user = ("spread", n)
                            if h == DOWN_SLOT and n:
                                down(n - 1)
                            if h == 0 and kt == 2 and j:
                                read_before(tr_user)
                                att_transpose(j - 1)
                                tr_user = ("att", j - 1)
                            if len(tiles) == 2:
                                next_score(tiles[1])
                down_shared(0)
                if more:
                    read_before(("up", SLICES - 1))
                    make_v(b + 1)
                pv(SLICES - 1)
                read_before(tr_user)
                if more:
                    gate_transpose(b + 1)
                down_shared(1)
                if more:
                    pe.wait_ge(v_ready, b + 2)
                    shared_up(0)
                if more:
                    pe.wait_ge(gT_ready, b + 2)
                att_transpose(NQ - 1)
                down(SLICES - 1)
                if more:
                    pe.wait_ge(sh_relu, (b + 1) * NSH + 1)
                    shared_up(1)
            over_batches(pe, batch)


def kernel(L0_attn_x, L0_attn_Wq, L0_attn_Wk, L0_attn_Wv, L0_ffn_gate_w, L0_ffn_e_bias, L0_ffn_up_w,
           L0_ffn_down_w, L0_ffn_shared_up_w, L0_ffn_shared_down_w):
    from concourse import bacc
    from concourse.bass_utils import run_bass_kernel_spmd

    half = HD // 2
    theta = 1.0 / 10000.0 ** (np.arange(0, HD, 2, dtype=np.float64) / HD)
    angle = np.arange(B, dtype=np.float64)[:, None] * theta[None, :]
    turn = np.concatenate([np.cos(angle) + np.sin(angle), np.cos(angle) - np.sin(angle)], axis=1)
    assert turn.shape == (B, 2 * half)
    rope = np.tile(np.stack([turn / np.sqrt(HD), turn], axis=1).reshape(2 * B, HD).T, (H, 1)).astype(np.float32)

    def lay(a):
        return np.ascontiguousarray(a)

    x = np.asarray(L0_attn_x)
    arrays = {
        "x": lay(x.reshape(B * T, D)),
        "wqT": lay(np.asarray(L0_attn_Wq).T),
        "wkT": lay(np.asarray(L0_attn_Wk).T),
        "wvT": lay(np.asarray(L0_attn_Wv).T),
        "gateT": lay(np.asarray(L0_ffn_gate_w).T),
        "e_bias": lay(np.asarray(L0_ffn_e_bias)),
        "upT": lay(np.asarray(L0_ffn_up_w).reshape(NE * EI, D).T),
        "down": lay(np.asarray(L0_ffn_down_w).transpose(0, 2, 1).reshape(NE * EI, D)),
        "shared_upT": lay(np.asarray(L0_ffn_shared_up_w).T),
        "shared_down": lay(np.asarray(L0_ffn_shared_down_w).T),
        "rope": lay(rope),
        "ident_d": np.eye(P, dtype=np.float32),
        "expert_rows": np.tile(np.eye(NE, dtype=np.float32), (PARTS, 1)),
        "head_rows": np.repeat(np.tile(np.eye(QUAD, dtype=np.float32), (PARTS, 1)), T // 2, axis=1) * TWO_ONES,
    }
    nc = bacc.Bacc("TRN2", target_bir_lowering=False, num_devices=1)
    args = [nc.dram_tensor(f"in_{n}", a.shape, mybir.dt.from_np(a.dtype), kind="ExternalInput").ap()
            for n, a in arrays.items()]
    out = nc.dram_tensor("out", (B * T, D), F32, kind="ExternalOutput").ap()
    build(nc, *args, out)
    r = run_bass_kernel_spmd(nc, [{f"in_{n}": a for n, a in arrays.items()}], core_ids=[0])
    return r.results[0]["out"].reshape(B, T, D)
```
